# Optimizing a Trainium2 kernel written in Bass

```python
import numpy as np
import jax
import jax.numpy as jnp

def _softmax(x, axis=-1):
    return jax.nn.softmax(x, axis=axis)

def _gelu(x):
    return jax.nn.gelu(x, approximate=True)

def _silu(x):
    return jax.nn.silu(x)

def _sigmoid(x):
    return jax.nn.sigmoid(x)

def _layernorm(x, axis=-1, eps=1e-05):
    m = jnp.mean(x, axis=axis, keepdims=True)
    v = jnp.var(x, axis=axis, keepdims=True)
    return (x - m) / jnp.sqrt(v + eps)

def _scatter_add(tgt, idx, src, axis=0):
    return tgt.at[idx].add(src)

def _segment_sum(src, seg, n):
    return jax.ops.segment_sum(src, seg, n)
kernel_name = 'mk_seq_postln_d1_jaxref_r8_8a362b'

def setup_inputs(seed: int=0):
    np.random.seed(seed)
    _w = jnp.asarray

    def _L0_attn_setup():
        import jax, jax.numpy as jnp
        import numpy as np
        import math
        N_HEAD = 16
        K_SPARSE = 64
        key = jax.random.key(seed)
        ks = jax.random.split(key, 12)
        B, T, C = (1, 256, 128)
        s = 0.02
        return {'x': jax.random.normal(ks[0], (B, T, C), jnp.float32), 'Wq': jax.random.normal(ks[1], (C, C), jnp.float32) * s, 'bq': jax.random.normal(ks[2], (C,), jnp.float32) * s, 'Wk': jax.random.normal(ks[3], (C, C), jnp.float32) * s, 'bk': jax.random.normal(ks[4], (C,), jnp.float32) * s, 'Wv': jax.random.normal(ks[5], (C, C), jnp.float32) * s, 'bv': jax.random.normal(ks[6], (C,), jnp.float32) * s, 'Wo': jax.random.normal(ks[7], (C, C), jnp.float32) * s, 'bo': jax.random.normal(ks[8], (C,), jnp.float32) * s, 'Wks': jax.random.normal(ks[9], (C,), jnp.float32) * s, 'bks': jax.random.normal(ks[10], (), jnp.float32) * s}
    _L0_attn_in = _L0_attn_setup()

    def _L0_ffn_setup():
        import jax, jax.numpy as jnp
        import numpy as np
        DIM = 128
        HIDDEN = 128
        NUM_EXPERTS = 8
        TOP_K = 2
        key = jax.random.key(seed)
        ks = jax.random.split(key, 8)
        std = 0.02
        x = jax.random.normal(ks[0], (2, 128, DIM), dtype=jnp.float32)
        gate_w = jax.random.normal(ks[1], (NUM_EXPERTS, DIM), dtype=jnp.float32) * std
        w1 = jax.random.normal(ks[2], (NUM_EXPERTS, DIM, HIDDEN), dtype=jnp.float32) * std
        w2 = jax.random.normal(ks[3], (NUM_EXPERTS, HIDDEN, DIM), dtype=jnp.float32) * std
        w3 = jax.random.normal(ks[4], (NUM_EXPERTS, DIM, HIDDEN), dtype=jnp.float32) * std
        w1s = jax.random.normal(ks[5], (1, DIM, HIDDEN), dtype=jnp.float32) * std
        w2s = jax.random.normal(ks[6], (1, HIDDEN, DIM), dtype=jnp.float32) * std
        w3s = jax.random.normal(ks[7], (1, DIM, HIDDEN), dtype=jnp.float32) * std
        return {'x': x, 'gate_w': gate_w, 'w1': w1, 'w2': w2, 'w3': w3, 'w1s': w1s, 'w2s': w2s, 'w3s': w3s}
    _L0_ffn_in = _L0_ffn_setup()
    _d = {'L0_attn_x': _L0_attn_in['x'], 'L0_attn_Wq': _L0_attn_in['Wq'], 'L0_attn_bq': _L0_attn_in['bq'], 'L0_attn_Wk': _L0_attn_in['Wk'], 'L0_attn_bk': _L0_attn_in['bk'], 'L0_attn_Wv': _L0_attn_in['Wv'], 'L0_attn_bv': _L0_attn_in['bv'], 'L0_attn_Wo': _L0_attn_in['Wo'], 'L0_attn_bo': _L0_attn_in['bo'], 'L0_attn_Wks': _L0_attn_in['Wks'], 'L0_attn_bks': _L0_attn_in['bks'], 'L0_ffn_gate_w': _L0_ffn_in['gate_w'], 'L0_ffn_w1': _L0_ffn_in['w1'], 'L0_ffn_w2': _L0_ffn_in['w2'], 'L0_ffn_w3': _L0_ffn_in['w3'], 'L0_ffn_w1s': _L0_ffn_in['w1s'], 'L0_ffn_w2s': _L0_ffn_in['w2s'], 'L0_ffn_w3s': _L0_ffn_in['w3s']}
    _x0 = _d['L0_attn_x']
    _d['L0_attn_x'] = jax.random.normal(jax.random.fold_in(jax.random.key(seed), 1), (16, 512, 128), dtype=_x0.dtype)
    del _x0
    return _d

def reference(L0_attn_x, L0_attn_Wq, L0_attn_bq, L0_attn_Wk, L0_attn_bk, L0_attn_Wv, L0_attn_bv, L0_attn_Wo, L0_attn_bo, L0_attn_Wks, L0_attn_bks, L0_ffn_gate_w, L0_ffn_w1, L0_ffn_w2, L0_ffn_w3, L0_ffn_w1s, L0_ffn_w2s, L0_ffn_w3s):

    def _L0_attn_ref(x, Wq, bq, Wk, bk, Wv, bv, Wo, bo, Wks, bks):
        import jax, jax.numpy as jnp
        import numpy as np
        import math
        N_HEAD = 16
        K_SPARSE = 64
        B, T, C = x.shape
        nh = N_HEAD
        hs = C // nh
        k_val = min(K_SPARSE, T)
        q = (x @ Wq.T + bq).reshape(B, T, nh, hs).transpose(0, 2, 1, 3)
        k = (x @ Wk.T + bk).reshape(B, T, nh, hs).transpose(0, 2, 1, 3)
        v = (x @ Wv.T + bv).reshape(B, T, nh, hs).transpose(0, 2, 1, 3)
        key_scores = x @ Wks + bks
        pos = jnp.arange(T)
        causal = pos[None, :] <= pos[:, None]
        masked = jnp.where(causal[None], key_scores[:, None, :], -jnp.inf)
        _, top_k_idx = jax.lax.top_k(masked, k_val)
        top_k_idx = jnp.minimum(top_k_idx, pos[None, :, None])
        bi = jnp.arange(B)[:, None, None, None]
        hi = jnp.arange(nh)[None, :, None, None]
        gi = top_k_idx[:, None, :, :]
        sparse_k = k[bi, hi, gi]
        sparse_v = v[bi, hi, gi]
        scale = 1.0 / math.sqrt(hs)
        logits = jnp.einsum('bhtd,bhtkd->bhtk', q, sparse_k) * scale
        probs = jax.nn.softmax(logits, axis=-1)
        out = jnp.einsum('bhtk,bhtkd->bhtd', probs, sparse_v)
        out = out.transpose(0, 2, 1, 3).reshape(B, T, C)
        return out @ Wo.T + bo

    def _L0_ffn_ref(x, gate_w, w1, w2, w3, w1s, w2s, w3s):
        import jax, jax.numpy as jnp
        import numpy as np
        DIM = 128
        HIDDEN = 128
        NUM_EXPERTS = 8
        TOP_K = 2
        bs, slen, dim = x.shape
        xt = x.reshape(bs * slen, dim)
        logits = xt @ gate_w.T
        scores = jax.nn.softmax(logits.astype(jnp.float32), axis=1).astype(x.dtype)
        top_scores, sel = jax.lax.top_k(scores, TOP_K)
        sel_flat = sel.reshape(-1)
        order = jnp.argsort(sel_flat, stable=True)
        top_scores_sorted = top_scores.reshape(-1)[order]
        token_idx = order // TOP_K
        eid = sel_flat[order]
        routed_in = xt[token_idx] * top_scores_sorted[:, None]
        out_routed = jnp.zeros_like(routed_in)
        for e in range(NUM_EXPERTS):
            m = (eid == e)[:, None]
            xe = jnp.where(m, routed_in, 0.0)
            h = jax.nn.silu(xe @ w1[e]) * (xe @ w3[e])
            out_routed = out_routed + jnp.where(m, h @ w2[e], 0.0)
        hs = jax.nn.silu(xt @ w1s[0]) * (xt @ w3s[0])
        out = hs @ w2s[0]
        out = out.at[token_idx].add(out_routed)
        return out.reshape(bs, slen, dim)
    x = L0_attn_x
    x = _layernorm(x + _L0_attn_ref(x, L0_attn_Wq, L0_attn_bq, L0_attn_Wk, L0_attn_bk, L0_attn_Wv, L0_attn_bv, L0_attn_Wo, L0_attn_bo, L0_attn_Wks, L0_attn_bks), axis=-1)
    x = _layernorm(x + _L0_ffn_ref(x, L0_ffn_gate_w, L0_ffn_w1, L0_ffn_w2, L0_ffn_w3, L0_ffn_w1s, L0_ffn_w2s, L0_ffn_w3s), axis=-1)
    return x

_drawn_inputs = setup_inputs


def setup_inputs(seed=0):
    import zlib

    import numpy as np

    out = dict(_drawn_inputs(seed))
    spreads = {}
    factors = {'L0_attn_Wq': 8.0,
     'L0_attn_bq': 8.0,
     'L0_attn_Wk': 8.0,
     'L0_attn_bk': 8.0,
     'L0_attn_Wv': 4.318,
     'L0_attn_bv': 8.0,
     'L0_attn_Wo': 3.986,
     'L0_attn_bo': 2.682,
     'L0_attn_Wks': 7.166,
     'L0_ffn_gate_w': 8.0,
     'L0_ffn_w1': 8.0,
     'L0_ffn_w2': 8.0,
     'L0_ffn_w3': 8.0,
     'L0_ffn_w1s': 8.0,
     'L0_ffn_w2s': 8.0,
     'L0_ffn_w3s': 8.0}
    for name, (base, spread) in spreads.items():
        noise = np.random.default_rng([zlib.crc32(name.encode()), seed]).standard_normal(out[name].shape)
        drawn = base * np.exp(spread * noise) if base else spread * noise
        out[name] = jnp.asarray(drawn.astype(out[name].dtype))
    for name, factor in factors.items():
        out[name] = (out[name] * factor).astype(out[name].dtype)
    return out
```

```python
from contextlib import ExitStack

import numpy as np

import concourse.bass as bass
from concourse import mybir

ALU = mybir.AluOpType
ACT = mybir.ActivationFunctionType
F32 = mybir.dt.float32
BF16 = mybir.dt.bfloat16
AX_X = mybir.AxisListType.X

P = 128
B, T, C = 16, 512, 128
HEADS = 16
HS = C // HEADS
KEEP = 64
QB = 64
NBLK = T // QB
NCAND = NBLK - 1
EXPERTS = 8
NE = EXPERTS + 1
HIDDEN = 128
TILES = T // P
SCALE = 1.0 / HS ** 0.5
EPS = 1e-5
MASKED = -1e30
KVS = 2 * C + 1
PAIRS = HEADS // 2
GRP = 4
SHARED = EXPERTS
ORDER = [SHARED] + list(range(EXPERTS))

CONST_PARTS = [("ident", P), ("seen", P), ("future", P), ("future0", P), ("before", P),
               ("slot", KEEP), ("times", QB), ("lower8", EXPERTS * EXPERTS), ("headsel", GRP)]


def shape_constants():
    r = np.arange(P)[:, None]
    c = np.arange(P)[None, :]
    u = r % QB
    t = {
        "ident": (r == c),
        "seen": (r < KEEP) | (r - KEEP <= c % QB),
        "future": KEEP * (c - KEEP > u),
        "future0": (c > u),
        "before": (r < c),
        "slot": np.broadcast_to(P - 1 - np.arange(KEEP), (P, KEEP)),
        "times": np.where(np.arange(QB)[None, :] == r, KEEP - np.arange(QB)[None, :], 1),
        "lower8": np.broadcast_to(np.tril(np.ones((EXPERTS, EXPERTS)), -1).reshape(1, -1), (P, EXPERTS ** 2)),
        "headsel": (np.arange(P)[:, None] // HS % GRP == np.arange(GRP)[None, :]),
    }
    return np.concatenate([np.asarray(t[n], np.float32).reshape(P, w) for n, w in CONST_PARTS], axis=1)


def post_ln_layer(nc, x, x_t, wq_t, bq, w_kvs, b_kvs, wo_t, bo, gate_t, w1, w3, w2, consts, out):
    gate_dram = nc.dram_tensor("gate_dram", (2, EXPERTS, T), F32, kind="Internal").ap()
    with ExitStack() as ctx:
        def sb(name, shape, dt=F32):
            return ctx.enter_context(nc.sbuf_tensor(name, shape, dt))

        def bank(name):
            return ctx.enter_context(nc.psum_tensor(name, [P, 512], F32))

        def sem(name):
            return ctx.enter_context(nc.semaphore(name))

        n_const = sum(w for _, w in CONST_PARTS)
        table = sb("table", [P, n_const])
        at, tables = 0, {}
        for n, w in CONST_PARTS:
            tables[n] = table[:, at:at + w]
            at += w
        ident = tables["ident"]
        ident_bf = sb("ident_bf", [P, P], BF16)
        negid_bf = sb("negid_bf", [P, P], BF16)
        seen_bf = sb("seen_bf", [P, P], BF16)
        future_bf = sb("future_bf", [P, P], BF16)
        ones32 = sb("ones32", [P, 32])
        wq_sb = sb("wq_sb", [P, C])
        bq_sb = sb("bq_sb", [P, 1])
        wkvs_sb = sb("wkvs_sb", [P, KVS])
        bias_all = sb("bias_all", [P, KVS])
        bias_new = sb("bias_new", [P, KVS])
        wo_sb = sb("wo_sb", [P, C])
        wo4 = sb("wo4", [P, GRP, C])
        bo_sb = sb("bo_sb", [P, C])
        gate_w = sb("gate_w", [P, EXPERTS])
        w1_sb = sb("w1_sb", [P, NE, HIDDEN])
        w3_sb = sb("w3_sb", [P, NE, HIDDEN])
        w2_sb = sb("w2_sb", [P, NE, C])
        xt_sb = sb("xt_sb", [P, 2, T])
        xn_sb = sb("xn_sb", [P, 2, TILES, C])
        q_sb = sb("q_sb", [P, 2, T])
        qb_sb = sb("qb_sb", [P, 2, T], BF16)
        qbd = sb("qbd", [P, 2, NBLK, HEADS, QB])
        qbd_bf = sb("qbd_bf", [P, 2, NBLK, HEADS, QB], BF16)
        kvs = sb("kvs", [P, NCAND, KVS])
        kt = sb("kt", [P, NCAND, P])
        kt_bf = sb("kt_bf", [P, NCAND, P], BF16)
        ties = sb("ties", [P, P])
        beats = sb("beats", [P, P], BF16)
        wins = sb("wins", [P, 1])
        perm = sb("perm", [P, KEEP])
        mask = sb("mask", [P, NBLK, P], BF16)
        rowmax = sb("rowmax", [P, 2, PAIRS], BF16)
        probs = sb("probs", [P, 2, HEADS, QB])
        rden = sb("den", [P, GRP, QB])
        attn = sb("attn", [P, GRP, 2, QB])
        z1 = sb("z1", [P, TILES, C])
        stats = sb("stats", [P, TILES, 6])
        mv = sb("mv", [P, TILES, 2])
        rstd = sb("rstd", [P, TILES])
        eps = sb("eps", [P, TILES])
        var = sb("var", [P, TILES])
        var2 = sb("var2", [P, TILES])
        minus_half = sb("minus_half", [P, TILES])
        x1 = sb("x1", [P, TILES, C])
        x1t = sb("x1t", [P, T])
        lmax = sb("lmax", [P, TILES])
        lsub = sb("lsub", [P, TILES, EXPERTS])
        lexp = sb("lexp", [P, TILES, EXPERTS])
        lsum = sb("lsum", [P, TILES])
        linv = sb("linv", [P, TILES])
        score = sb("score", [P, TILES, EXPERTS])
        better = sb("better", [P, TILES, EXPERTS, EXPERTS])
        equal = sb("equal", [P, TILES, EXPERTS, EXPERTS])
        rank8 = sb("rank8", [P, TILES, EXPERTS])
        gate = sb("gate", [P, TILES, EXPERTS])
        gate_rows = sb("gate_rows", [EXPERTS, T])
        gate_b = sb("gate_b", [P, EXPERTS, T])
        xe = sb("xe", [P, 2, T])
        act_g = sb("act_g", [P, 2, T])
        hid = sb("hid", [P, 2, T])
        z2 = sb("z2", [P, TILES, C])
        stats2 = sb("stats2", [P, TILES, 6])
        mv2 = sb("mv2", [P, TILES, 2])
        rstd2 = sb("rstd2", [P, TILES])
        y_sb = sb("y_sb", [P, 2, TILES, C])

        bank_a = [bank("bank_a0"), bank("bank_a1")]
        bank_b = [bank("bank_b0"), bank("bank_b1")]
        bank_kv = bank("bank_kv")
        bank_t = bank("bank_t")
        bank_o = bank("bank_o")
        bank_y = bank("bank_y")
        gu_banks = [bank_a, bank_b]

        weights_in = sem("weights_in")
        x_in = [sem("x_in0"), sem("x_in1")]
        qbd_in = [sem("qbd_in0"), sem("qbd_in1")]
        gate_out = sem("gate_out")
        gate_in = sem("gate_in")
        y_out = [sem("y_out0"), sem("y_out1")]
        tables_bf = sem("tables_bf")
        zeroed = sem("zeroed")
        q_done = sem("q_done")
        kv_done = sem("kv_done")
        tp_done = sem("tp_done")
        count_done = sem("count_done")
        a_done = sem("a_done")
        b_done = sem("b_done")
        o_done = sem("o_done")
        y_done = sem("y_done")
        x1t_done = sem("x1t_done")
        logit_done = sem("logit_done")
        gatet_done = sem("gatet_done")
        g_done = sem("g_done")
        u_done = sem("u_done")
        ffn_done = sem("ffn_done")
        q_ready = sem("q_ready")
        kt_ready = sem("kt_ready")
        exp_done = sem("exp_done")
        x1t_ready = sem("x1t_ready")
        lexp_ready = sem("lexp_ready")
        gate_rows_ready = sem("gate_rows_ready")
        silu_done = sem("silu_done")
        kvs_ready = sem("kvs_ready")
        ties_done = sem("ties_done")
        beats_ready = sem("beats_ready")
        perm_ready = sem("perm_ready")
        mask_ready = sem("mask_ready")
        max_ready = sem("max_ready")
        weighted = sem("weighted")
        rden_done = sem("rden_done")
        attn_ready = sem("attn_ready")
        z1_ready = sem("z1_ready")
        stats_done = sem("stats_done")
        mv_ready = sem("mv_ready")
        x1_ready = sem("x1_ready")
        gate_step = sem("gate_step")
        lsub_ready = sem("lsub_ready")
        gate_ready = sem("gate_ready")
        xe_ready = sem("xe_ready")
        hid_ready = sem("hid_ready")
        z2_ready = sem("z2_ready")
        stats2_done = sem("stats2_done")
        mv2_ready = sem("mv2_ready")
        stats_seen = sem("stats_seen")
        y_ready = sem("y_ready")
        res_ready = sem("res_ready")
        half_set = sem("half_set")
        var_done = sem("var_done")
        var2_done = sem("var2_done")
        rstd_ready = sem("rstd_ready")
        rstd2_ready = sem("rstd2_ready")

        block = ctx.enter_context(nc.Block())
        N_WEIGHTS = 12

        @block.sync
        def _(sp):
            loads = [(table[:], consts), (wq_sb[:], wq_t), (bq_sb[:], bq), (wkvs_sb[:], w_kvs),
                     (bias_all[:], b_kvs.to_broadcast([P, KVS])),
                     (bias_new[KEEP:P, :], b_kvs.to_broadcast([P - KEEP, KVS])),
                     (wo_sb[:], wo_t), (bo_sb[:], bo.to_broadcast([P, C])), (gate_w[:], gate_t),
                     (w1_sb[:], w1), (w3_sb[:], w3), (w2_sb[:], w2)]

            def load_x(b, half):
                sp.dma_start(xt_sb[:, half, :], x_t[b]).then_inc(x_in[half], 16)
                sp.dma_start(xn_sb[:, half, :, :], x[b].rearrange("(t p) c -> p t c", p=P)).then_inc(x_in[half], 16)

            load_x(0, 0)
            for dst, src in loads:
                sp.dma_start(dst, src).then_inc(weights_in, 16)
            sp.wait_ge(zeroed, 4)

            def sequence(i, half, prefetch):
                b = 2 * i + half
                sp.wait_ge(q_ready, b + 1)
                for src, dst in ((q_sb, qbd), (qb_sb, qbd_bf)):
                    for h in range(HEADS):
                        rows = slice(h * HS, (h + 1) * HS)
                        sp.dma_start(dst[rows, half, :, h, :],
                                     src[rows, half, :].rearrange("p (k q) -> p k q", q=QB)).then_inc(qbd_in[half], 16)
                if prefetch:
                    load_x(b + 1, 1 - half)
                sp.wait_ge(gate_rows_ready, b + 2)
                sp.dma_start(gate_dram[half], gate_rows[:]).then_inc(gate_out, 16)
                sp.wait_ge(gate_out, 16 * b + 16)
                sp.dma_start(gate_b[:].rearrange("p e t -> p (e t)"),
                             gate_dram[half].rearrange("e t -> (e t)").partition_broadcast(P)).then_inc(gate_in, 16)
                sp.wait_ge(y_ready, b + 1)
                sp.dma_start(out[b].rearrange("(t p) c -> p t c", p=P), y_sb[:, half, :, :]).then_inc(y_out[half], 16)

            with sp.Fori(0, B // 2 - 1) as i:
                for half in range(2):
                    sequence(i, half, True)
            for half in range(2):
                sequence(B // 2 - 1, half, half == 0)
            for half in range(2):
                sp.wait_ge(y_out[half], 16 * (B // 2))

        @block.gpsimd
        def _(pool):
            pool.memset(qbd[:, 1], 0.0).then_inc(zeroed, 1)
            pool.memset(qbd_bf[:, 1], 0.0).then_inc(zeroed, 1)
            pool.memset(minus_half[:], -0.5).then_inc(half_set, 1)
            pool.memset(eps[:], EPS).then_inc(half_set, 1)
            pool.wait_ge(half_set, 2)
            pool.wait_ge(weights_in, 16 * N_WEIGHTS)
            with pool.Fori(0, B // 2) as i:
                for half in range(2):
                    b = 2 * i + half
                    pool.wait_ge(x_in[half], 32 * i + 32)
                    pool.tensor_tensor(xn_sb[:, half], xn_sb[:, half],
                                       bo_sb[:].unsqueeze(1).to_broadcast([P, TILES, C]), ALU.add).then_inc(res_ready, 1)
                    pool.wait_ge(mv_ready, b + 1)
                    pool.tensor_tensor(var[:], mv[:, :, 1], eps[:], ALU.add).then_inc(var_done, 1)
                    pool.wait_ge(var_done, b + 1)
                    pool.tensor_tensor(rstd[:], var[:], minus_half[:], ALU.pow).then_inc(rstd_ready, 1)
                    pool.wait_ge(mv2_ready, b + 1)
                    pool.tensor_tensor(var2[:], mv2[:, :, 1], eps[:], ALU.add).then_inc(var2_done, 1)
                    pool.wait_ge(var2_done, b + 1)
                    pool.tensor_tensor(rstd2[:], var2[:], minus_half[:], ALU.pow).then_inc(rstd2_ready, 1)

        @block.tensor
        def _(pe):
            def mm(out_, lhs, rhs, start=True, stop=True):
                return pe.matmul(out_, lhs, rhs, start=start, stop=stop, skip_group_check=True)

            pe.wait_ge(weights_in, 16 * N_WEIGHTS)
            pe.wait_ge(tables_bf, 1)

            def sequence(i, half):
                b = 2 * i + half

                def queries():
                    pe.wait_ge(x_in[half], 32 * i + 32)
                    pe.wait_ge(gate_rows_ready, b + 1)
                    mm(bank_y[:], wq_sb[:], xt_sb[:, half, :]).then_inc(q_done, 1)

                def project(c):
                    if c == 1:
                        pe.wait_ge(z2_ready, b + 1)
                        mm(bank_kv[:, 0:KVS], xt_sb[:, half, 0:P], wkvs_sb[:]).then_inc(kv_done, 1)
                        return
                    pe.wait_ge(perm_ready, (NCAND - 1) * b + c - 1)
                    mm(bank_kv[KEEP:P, 0:KVS], xt_sb[:, half, QB * c:QB * (c + 1)], wkvs_sb[:])
                    mm(bank_kv[0:KEEP, 0:KVS], perm[:], kvs[:, c - 2, :]).then_inc(kv_done, 1)

                def turn(c):
                    pe.wait_ge(kvs_ready, NCAND * b + c)
                    pe.wait_ge(mask_ready, NCAND * b + c)
                    pe.transpose(bank_t[:, 0:P], kvs[:, c - 1, 0:C], ident)
                    pe.transpose(bank_kv[:, 3 * P:4 * P], kvs[:, c - 1, 2 * C:KVS].to_broadcast([P, P]),
                                 ident).then_inc(tp_done, 1)

                def count(c):
                    pe.wait_ge(kt_ready, NCAND * b + c)
                    pe.wait_ge(beats_ready, NCAND * b + c)
                    mm(bank_t[:, 2 * P:3 * P], seen_bf[:], beats[:], stop=False)
                    mm(bank_t[:, 2 * P:3 * P], ident_bf[:], future_bf[:], start=False).then_inc(count_done, 1)

                def logits_a(k):
                    c = max(k, 1) - 1
                    if k == 0:
                        pe.wait_ge(qbd_in[half], 32 * 16 * (i + 1))
                        pe.wait_ge(kt_ready, NCAND * b + 1)
                        pe.wait_ge(hid_ready, NE * b + 1)
                    else:
                        pe.wait_ge(mask_ready, NCAND * b + k + 1)
                    for g in range(2):
                        if k > 0:
                            pe.wait_ge(max_ready, 2 * NBLK * b + 2 * (k - 1) + g + 1)
                        mm(bank_a[g][:], ident_bf[:], mask[:, k, :].unsqueeze(1).to_broadcast([P, 4, P]), stop=False)
                        for p in range(4):
                            last = mm(bank_a[g][:, p * P:(p + 1) * P],
                                      qbd_bf[:, half, k, 8 * g + 2 * p:8 * g + 2 * p + 2, :].rearrange("p h q -> p (h q)"),
                                      kt_bf[:, c, :], start=False, stop=p == 3)
                        last.then_inc(a_done, 1)

                def logits_b(k):
                    c = max(k, 1) - 1
                    for g in range(2):
                        if k > 0:
                            pe.wait_ge(exp_done, 2 * NBLK * b + 2 * (k - 1) + g + 1)
                        mm(bank_b[g][:], kt[:, c, :], qbd[:, half, k, 8 * g:8 * g + 8, :].rearrange("p h q -> p (h q)"),
                           stop=False)
                        mm(bank_b[g][:], mask[:, k, :], ident_bf[:].unsqueeze(1).to_broadcast([P, 4, P]),
                           start=False, stop=False)
                        pe.wait_ge(max_ready, 2 * NBLK * b + 2 * k + g + 1)
                        for p in range(4):
                            last = mm(bank_b[g][:, p * P:(p + 1) * P],
                                      rowmax[:, k % 2, 4 * g + p:4 * g + p + 1].to_broadcast([P, P]),
                                      negid_bf[:], start=False, stop=p == 3)
                        last.then_inc(b_done, 1)

                def values(k):
                    c = max(k, 1) - 1
                    pe.wait_ge(attn_ready, NBLK * b + k + 1)
                    pe.wait_ge(exp_done, 2 * NBLK * b + 2 * k + 2)
                    if k == 0:
                        pe.wait_ge(weighted, b + 1)
                    for g in range(GRP):
                        e = probs[:, k % 2, 4 * g:4 * g + 4, :].rearrange("p h q -> p (h q)")
                        mm(bank_o[32 * g:32 * g + 32, 0:256], kvs[:, c, C + 32 * g:C + 32 * g + 32], e)
                    for g in range(GRP):
                        e = probs[:, k % 2, 4 * g:4 * g + 4, :].rearrange("p h q -> p (h q)")
                        last = mm(bank_o[32 * g:32 * g + 32, 256:512], ones32[:], e)
                    last.then_inc(o_done, 1)

                def project_out(j):
                    pe.wait_ge(attn_ready, NBLK * b + 2 * j + 3)
                    if j == 0:
                        pe.wait_ge(q_ready, b + 1)
                    else:
                        pe.wait_ge(z1_ready, TILES * b + j)
                    for h in range(GRP):
                        last = mm(bank_y[:, 0:C], attn[:, h].rearrange("p k q -> p (k q)"), wo4[:, h, :],
                                  start=h == 0, stop=h == GRP - 1)
                    last.then_inc(y_done, 1)

                queries()
                project(1)
                turn(1)
                for k in range(NBLK + 3):
                    if k < NBLK:
                        logits_a(k)
                    if k + 1 <= NCAND:
                        count(k + 1)
                    if k + 2 <= NCAND:
                        project(k + 2)
                    if 0 <= k - 1 < NBLK:
                        logits_b(k - 1)
                    if k + 2 <= NCAND:
                        turn(k + 2)
                    if k >= 4 and k % 2 == 0:
                        project_out(k // 2 - 2)
                    if 0 <= k - 2 < NBLK:
                        values(k - 2)

                pe.wait_ge(x1_ready, b + 1)
                for t in range(TILES):
                    last = pe.transpose(bank_y[:, t * P:(t + 1) * P], x1[:, t, :], ident)
                last.then_inc(x1t_done, 1)
                pe.wait_ge(x1t_ready, b + 1)
                for t in range(TILES):
                    last = mm(bank_y[:, EXPERTS * t:EXPERTS * (t + 1)], x1t[:, t * P:(t + 1) * P], gate_w[:])
                last.then_inc(logit_done, 1)

                def up(n):
                    e = ORDER[n]
                    if n < 2:
                        pe.wait_ge([max_ready, exp_done][n], 2 * NBLK * b + 2 * NBLK)
                    else:
                        pe.wait_ge(hid_ready, NE * b + n)
                    if n > 0:
                        pe.wait_ge(xe_ready, EXPERTS * b + n)
                    src = x1t[:] if n == 0 else xe[:, n % 2, :]
                    mm(gu_banks[n % 2][0][:], w1_sb[:, e, :], src).then_inc(g_done, 1)
                    mm(gu_banks[n % 2][1][:], w3_sb[:, e, :], src).then_inc(u_done, 1)

                def down(n):
                    e = ORDER[n]
                    pe.wait_ge(hid_ready, NE * b + n + 2)
                    for t in range(TILES):
                        last = mm(bank_kv[:, t * C:(t + 1) * C], hid[:, n % 2, t * P:(t + 1) * P], w2_sb[:, e, :],
                                  start=n == 0 and t == 0, stop=n == NE - 1)
                    return last

                up(0)
                pe.wait_ge(gate_ready, b + 1)
                for t in range(TILES):
                    last = pe.transpose(bank_y[0:EXPERTS, t * P:(t + 1) * P], gate[:, t, :], ident)
                last.then_inc(gatet_done, 1)
                for n in range(1, NE):
                    up(n)
                    down(n - 1)
                down(NE - 1).then_inc(ffn_done, 1)

            with pe.Fori(0, B // 2) as i:
                for half in range(2):
                    sequence(i, half)

        @block.scalar
        def _(act):
            act.sem_inc(gate_rows_ready, 1)
            act.wait_ge(weights_in, 16 * N_WEIGHTS)

            def sequence(i, half):
                b = 2 * i + half
                act.wait_ge(q_done, b + 1)
                act.activation(q_sb[:, half, :], bank_y[:], ACT.Identity, bias=bq_sb[:])
                act.activation(qb_sb[:, half, :], bank_y[:], ACT.Identity, bias=bq_sb[:]).then_inc(q_ready, 1)

                def keys(c):
                    act.wait_ge(tp_done, NCAND * b + c)
                    act.activation(kt_bf[:, c - 1, :], bank_t[:, 0:P], ACT.Copy)
                    act.activation(kt[:, c - 1, :], bank_t[:, 0:P], ACT.Copy).then_inc(kt_ready, 1)

                def exps(k):
                    for g in range(2):
                        act.wait_ge(b_done, 2 * NBLK * b + 2 * k + g + 1)
                        act.activation(probs[:, k % 2, 8 * g:8 * g + 8, :].rearrange("p h q -> p (h q)"),
                                       bank_b[g][:], ACT.Exp, scale=SCALE).then_inc(exp_done, 1)

                keys(1)
                for k in range(NBLK + 1):
                    if 0 <= k - 1 < NBLK:
                        exps(k - 1)
                    if k + 2 <= NCAND:
                        keys(k + 2)
                act.wait_ge(x1t_done, b + 1)
                act.activation(x1t[:], bank_y[:], ACT.Copy).then_inc(x1t_ready, 1)
                act.wait_ge(lsub_ready, b + 1)
                act.activation(lexp[:], lsub[:], ACT.Exp).then_inc(lexp_ready, 1)

                def silu(n):
                    act.wait_ge(g_done, NE * b + n + 1)
                    act.activation(act_g[:, n % 2, :], gu_banks[n % 2][0][:], ACT.Silu).then_inc(silu_done, 1)

                silu(0)
                act.wait_ge(gatet_done, b + 1)
                act.activation(gate_rows[:], bank_y[0:EXPERTS, :], ACT.Copy).then_inc(gate_rows_ready, 1)
                for n in range(1, NE):
                    silu(n)

            with act.Fori(0, B // 2) as i:
                for half in range(2):
                    sequence(i, half)

        @block.vector
        def _(dve):
            dve.memset(qbd[:, 0], 0.0).then_inc(zeroed, 1)
            dve.memset(qbd_bf[:, 0], 0.0).then_inc(zeroed, 1)
            dve.memset(ones32[:], 1.0)
            dve.memset(bias_new[0:KEEP, :], 0.0)
            dve.wait_ge(weights_in, 16 * N_WEIGHTS)
            dve.tensor_copy(ident_bf[:], ident)
            dve.tensor_scalar(negid_bf[:], ident, -1.0, None, ALU.mult)
            dve.tensor_copy(seen_bf[:], tables["seen"])
            dve.tensor_copy(future_bf[:], tables["future"])
            dve.tensor_scalar(mask[:, 0, :], tables["future0"], MASKED, None, ALU.mult)
            for h in range(GRP):
                last = dve.tensor_scalar(wo4[:, h, :], wo_sb[:], tables["headsel"][:, h:h + 1], None, ALU.mult)
            last.then_inc(tables_bf, 1)
            for s in (mask_ready, attn_ready, hid_ready, z2_ready):
                dve.sem_inc(s, 1)

            def sequence(i, half):
                b = 2 * i + half

                def candidates(c):
                    dve.wait_ge(kv_done, NCAND * b + c)
                    bias = bias_all if c == 1 else bias_new
                    dve.tensor_tensor(kvs[:, c - 1, :], bank_kv[:, 0:KVS], bias[:], ALU.add).then_inc(kvs_ready, 1)

                def ranks(c):
                    dve.wait_ge(tp_done, NCAND * b + c)
                    own = kvs[:, c - 1, 2 * C:KVS]
                    dve.scalar_tensor_tensor(ties[:], bank_kv[:, 3 * P:4 * P], own, tables["before"],
                                             ALU.is_equal, ALU.mult).then_inc(ties_done, 1)
                    dve.wait_ge(ties_done, NCAND * b + c)
                    dve.scalar_tensor_tensor(beats[:], bank_kv[:, 3 * P:4 * P], own, ties[:],
                                             ALU.is_lt, ALU.add, accum_out=wins[:]).then_inc(beats_ready, 1)
                    if c < NCAND:
                        dve.wait_ge(beats_ready, NCAND * b + c)
                        dve.tensor_scalar(perm[:], tables["slot"], wins[:], None, ALU.is_equal).then_inc(perm_ready, 1)

                def masks(c):
                    dve.wait_ge(count_done, NCAND * b + c)
                    dve.tensor_scalar(mask[:, c, :], bank_t[:, 2 * P:3 * P], KEEP - 0.5, MASKED,
                                      ALU.is_ge, ALU.mult).then_inc(mask_ready, 1)

                def maxima(k):
                    for g in range(2):
                        dve.wait_ge(a_done, 2 * NBLK * b + 2 * k + g + 1)
                        dve.tensor_reduce(rowmax[:, k % 2, 4 * g:4 * g + 4],
                                          bank_a[g][:].rearrange("p (a j) -> p a j", a=4), AX_X,
                                          ALU.max).then_inc(max_ready, 1)

                def weigh():
                    dve.wait_ge(exp_done, 2 * NBLK * b + 2)
                    e = probs[0:QB, 0, :, :]
                    dve.tensor_tensor(e, e, tables["times"][0:QB, :].unsqueeze(1).to_broadcast([QB, HEADS, QB]),
                                      ALU.mult).then_inc(weighted, 1)

                def normalise(k):
                    dve.wait_ge(o_done, NBLK * b + k + 1)
                    dve.reciprocal(rden[:].rearrange("p h q -> p (h q)"), bank_o[:, 256:512]).then_inc(rden_done, 1)
                    dve.wait_ge(rden_done, NBLK * b + k + 1)
                    dve.tensor_tensor(attn[:, :, k % 2, :], bank_o[:, 0:256].rearrange("p (h q) -> p h q", h=GRP),
                                      rden[:], ALU.mult).then_inc(attn_ready, 1)

                def residual(j):
                    dve.wait_ge(y_done, TILES * b + j + 1)
                    if j == 0:
                        dve.wait_ge(res_ready, b + 1)
                    dve.tensor_tensor(z1[:, j, :], bank_y[:, 0:C], xn_sb[:, half, j, :], ALU.add).then_inc(z1_ready, 1)

                candidates(1)
                ranks(1)
                for k in range(NBLK + 3):
                    if k < NBLK:
                        maxima(k)
                    if k + 1 <= NCAND:
                        masks(k + 1)
                    if k + 2 <= NCAND:
                        candidates(k + 2)
                        ranks(k + 2)
                    if k == 1:
                        weigh()
                    if k >= 4 and k % 2 == 0:
                        residual(k // 2 - 2)
                    if 0 <= k - 2 < NBLK:
                        normalise(k - 2)

                def layernorm(z, z_sem, z_count, st, st_sem, mv_, mv_sem, rstd_, rstd_sem, dst, dst_sem):
                    dve.wait_ge(z_sem, z_count)
                    for t in range(TILES):
                        dve.bn_stats(st[:, t, :], z[:, t, :]).then_inc(st_sem, 1)
                    dve.wait_ge(st_sem, TILES * b + TILES)
                    dve.sem_inc(stats_seen, 1)
                    for t in range(TILES):
                        last = dve.bn_aggr(mv_[:, t, :], st[:, t, :])
                    last.then_inc(mv_sem, 1)
                    dve.wait_ge(rstd_sem, b + 1)
                    for t in range(TILES):
                        last = dve.tensor_scalar(dst[:, t, :], z[:, t, :], mv_[:, t, 0:1], rstd_[:, t:t + 1],
                                                 ALU.subtract, ALU.mult)
                    last.then_inc(dst_sem, 1)

                layernorm(z1, z1_ready, TILES * b + TILES, stats, stats_done, mv, mv_ready, rstd, rstd_ready,
                          x1, x1_ready)

                steps = [0]

                def step(ins):
                    steps[0] += 1
                    ins.then_inc(gate_step, 1)
                    dve.wait_ge(gate_step, 9 * b + steps[0])

                logits = bank_y[:, 0:TILES * EXPERTS].rearrange("p (t e) -> p t e", e=EXPERTS)
                over_e = [P, TILES, EXPERTS]
                over_ee = [P, TILES, EXPERTS, EXPERTS]
                dve.wait_ge(logit_done, b + 1)
                step(dve.tensor_reduce(lmax[:], logits, AX_X, ALU.max))
                dve.tensor_tensor(lsub[:], logits, lmax[:].unsqueeze(2).to_broadcast(over_e),
                                  ALU.subtract).then_inc(lsub_ready, 1)
                dve.wait_ge(lexp_ready, b + 1)
                step(dve.tensor_reduce(lsum[:], lexp[:], AX_X, ALU.add))
                step(dve.reciprocal(linv[:], lsum[:]))
                step(dve.tensor_tensor(score[:], lexp[:], linv[:].unsqueeze(2).to_broadcast(over_e), ALU.mult))
                other = score[:].unsqueeze(2).to_broadcast(over_ee)
                own = score[:].unsqueeze(3).to_broadcast(over_ee)
                step(dve.tensor_tensor(equal[:], other, own, ALU.is_equal))
                step(dve.tensor_tensor(equal[:].rearrange("p t e f -> p t (e f)"),
                                       equal[:].rearrange("p t e f -> p t (e f)"),
                                       tables["lower8"].unsqueeze(1).to_broadcast([P, TILES, EXPERTS ** 2]), ALU.mult))
                step(dve.tensor_tensor(better[:], other, own, ALU.is_gt))
                step(dve.tensor_tensor(better[:], better[:], equal[:], ALU.add))
                step(dve.tensor_reduce(rank8[:], better[:], AX_X, ALU.add))
                dve.scalar_tensor_tensor(gate[:], rank8[:], 1.5, score[:], ALU.is_lt, ALU.mult).then_inc(gate_ready, 1)

                def scale_x(n):
                    if n == 1:
                        dve.wait_ge(gate_in, 16 * b + 16)
                    dve.tensor_tensor(xe[:, n % 2, :], x1t[:], gate_b[:, ORDER[n], :], ALU.mult).then_inc(xe_ready, 1)

                def hidden(n):
                    dve.wait_ge(silu_done, NE * b + n + 1)
                    dve.wait_ge(u_done, NE * b + n + 1)
                    dve.tensor_tensor(hid[:, n % 2, :], gu_banks[n % 2][1][:], act_g[:, n % 2, :],
                                      ALU.mult).then_inc(hid_ready, 1)

                hidden(0)
                scale_x(1)
                scale_x(2)
                for n in range(1, NE):
                    hidden(n)
                    if n + 2 < NE:
                        scale_x(n + 2)
                dve.wait_ge(ffn_done, b + 1)
                dve.tensor_tensor(z2[:], bank_kv[:].rearrange("p (t c) -> p t c", c=C), x1[:],
                                  ALU.add).then_inc(z2_ready, 1)
                layernorm(z2, z2_ready, b + 2, stats2, stats2_done, mv2, mv2_ready, rstd2, rstd2_ready,
                          y_sb[:, half], y_ready)

            with dve.Fori(0, B // 2) as i:
                for half in range(2):
                    sequence(i, half)


def kernel(**inputs):
    import concourse.bacc as bacc
    from concourse.bass_utils import run_bass_kernel_spmd

    a = {k.replace("L0_", ""): np.asarray(v) for k, v in inputs.items()}
    experts = {n: np.concatenate([a[f"ffn_{n}"], a[f"ffn_{n}s"]]) for n in ("w1", "w3", "w2")}
    arrays = {
        "x": a["attn_x"],
        "x_t": a["attn_x"].transpose(0, 2, 1),
        "wq_t": a["attn_Wq"].T,
        "bq": a["attn_bq"][:, None],
        "w_kvs": np.concatenate([a["attn_Wk"].T, a["attn_Wv"].T, a["attn_Wks"][:, None]], axis=1),
        "b_kvs": np.concatenate([a["attn_bk"], a["attn_bv"], a["attn_bks"].reshape(1)])[None, :],
        "wo_t": a["attn_Wo"].T,
        "bo": a["attn_bo"][None, :],
        "gate_t": a["ffn_gate_w"].T,
        "w1": experts["w1"].transpose(1, 0, 2),
        "w3": experts["w3"].transpose(1, 0, 2),
        "w2": experts["w2"].transpose(1, 0, 2),
        "consts": shape_constants(),
    }
    nc = bacc.Bacc("TRN2", target_bir_lowering=False, num_devices=1)
    arrays = {f"in_{n}": np.ascontiguousarray(v) for n, v in arrays.items()}
    args = [nc.dram_tensor(n, v.shape, mybir.dt.from_np(v.dtype), kind="ExternalInput").ap() for n, v in arrays.items()]
    args.append(nc.dram_tensor("out_y", (B, T, C), F32, kind="ExternalOutput").ap())
    post_ln_layer(nc, *args)
    r = run_bass_kernel_spmd(nc, [arrays], core_ids=[0])
    return r.results[0]["out_y"]
```

```python
from contextlib import ExitStack

import numpy as np

import concourse.bass as bass
from concourse import mybir

ALU = mybir.AluOpType
ACT = mybir.ActivationFunctionType
F32 = mybir.dt.float32
BF16 = mybir.dt.bfloat16
AX_X = mybir.AxisListType.X

P = 128
B, T, C = 16, 512, 128
HEADS = 16
HS = C // HEADS
KEEP = 64
QB = 64
NBLK = T // QB
NCAND = NBLK - 1
EXPERTS = 8
NE = EXPERTS + 1
HIDDEN = 128
TILES = T // P
SCALE = 1.0 / HS ** 0.5
EPS = 1e-5
MASKED = -1e30
KVS = 2 * C + 1
PAIRS = HEADS // 2
GRP = 4
SHARED = EXPERTS
ORDER = [SHARED] + list(range(EXPERTS))

CONST_PARTS = [("ident", P), ("seen", P), ("future", P), ("future0", P), ("before", P),
               ("slot", KEEP), ("times", QB), ("lower8", EXPERTS * EXPERTS), ("odd", 2)]


def shape_constants():
    r = np.arange(P)[:, None]
    c = np.arange(P)[None, :]
    u = r % QB
    t = {
        "ident": (r == c),
        "seen": (r < KEEP) | (r - KEEP <= c % QB),
        "future": KEEP * (c - KEEP > u),
        "future0": (c > u),
        "before": (r < c),
        "slot": np.broadcast_to(P - 1 - np.arange(KEEP), (P, KEEP)),
        "times": np.where(np.arange(QB)[None, :] == r, KEEP - np.arange(QB)[None, :], 1),
        "lower8": np.broadcast_to(np.tril(np.ones((EXPERTS, EXPERTS)), -1).reshape(1, -1), (P, EXPERTS ** 2)),
        "odd": (np.arange(P)[:, None] // HS % 2 == np.arange(2)[None, :]),
    }
    return np.concatenate([np.asarray(t[n], np.float32).reshape(P, w) for n, w in CONST_PARTS], axis=1)


def post_ln_layer(nc, x, x_t, wq_t, bq, w_kvs, b_kvs, wo_t, bo, gate_t, w1, w3, w2, consts, out):
    gate_dram = nc.dram_tensor("gate_dram", (2, EXPERTS, T), F32, kind="Internal").ap()
    with ExitStack() as ctx:
        def sb(name, shape, dt=F32):
            return ctx.enter_context(nc.sbuf_tensor(name, shape, dt))

        def bank(name):
            return ctx.enter_context(nc.psum_tensor(name, [P, 512], F32))

        def sem(name):
            return ctx.enter_context(nc.semaphore(name))

        n_const = sum(w for _, w in CONST_PARTS)
        table = sb("table", [P, n_const])
        at, tables = 0, {}
        for n, w in CONST_PARTS:
            tables[n] = table[:, at:at + w]
            at += w
        ident = tables["ident"]
        ident_bf = sb("ident_bf", [P, P], BF16)
        negid_bf = sb("negid_bf", [P, P], BF16)
        seen_bf = sb("seen_bf", [P, P], BF16)
        future_bf = sb("future_bf", [P, P], BF16)
        ones_pair = sb("ones_pair", [P, 2, 32])
        wq_sb = sb("wq_sb", [P, C])
        bq_sb = sb("bq_sb", [P, 1])
        wkvs_sb = sb("wkvs_sb", [P, KVS])
        bias_all = sb("bias_all", [P, KVS])
        bias_new = sb("bias_new", [P, KVS])
        wo_sb = sb("wo_sb", [P, C])
        wo2 = sb("wo2", [P, 2, C])
        bo_sb = sb("bo_sb", [P, C])
        gate_w = sb("gate_w", [P, EXPERTS])
        w1_sb = sb("w1_sb", [P, NE, HIDDEN])
        w3_sb = sb("w3_sb", [P, NE, HIDDEN])
        w2_sb = sb("w2_sb", [P, NE, C])
        xt_sb = sb("xt_sb", [P, 2, T])
        xn_sb = sb("xn_sb", [P, 2, TILES, C])
        q_sb = sb("q_sb", [P, 2, T])
        qb_sb = sb("qb_sb", [P, 2, T], BF16)
        qbd = sb("qbd", [P, NBLK, HEADS, QB])
        qbd_bf = sb("qbd_bf", [P, NBLK, HEADS, QB], BF16)
        kvs = sb("kvs", [P, NCAND, KVS])
        vals = sb("vals", [P, NCAND, 2, C])
        kt = sb("kt", [P, NCAND, P])
        kt_bf = sb("kt_bf", [P, NCAND, P], BF16)
        ties = sb("ties", [P, P])
        beats = sb("beats", [P, P], BF16)
        wins = sb("wins", [P, 1])
        perm = sb("perm", [P, KEEP])
        mask = sb("mask", [P, NBLK, P], BF16)
        rowmax = sb("rowmax", [P, 2, PAIRS], BF16)
        probs = sb("probs", [P, 2, HEADS, QB])
        rden = sb("rden", [P, 2, QB])
        attn = sb("attn", [P, 2, 2, QB])
        z1 = sb("z1", [P, TILES, C])
        stats = sb("stats", [P, TILES, 6])
        mv = sb("mv", [P, TILES, 2])
        rstd = sb("rstd", [P, TILES])
        eps = sb("eps", [P, TILES])
        var = sb("var", [P, TILES])
        var2 = sb("var2", [P, TILES])
        minus_half = sb("minus_half", [P, TILES])
        x1 = sb("x1", [P, 2, TILES, C])
        x1t = sb("x1t", [P, 2, T])
        lmax = sb("lmax", [P, TILES])
        lsub = sb("lsub", [P, TILES, EXPERTS])
        lexp = sb("lexp", [P, TILES, EXPERTS])
        lsum = sb("lsum", [P, TILES])
        linv = sb("linv", [P, TILES])
        score = sb("score", [P, TILES, EXPERTS])
        better = sb("better", [P, TILES, EXPERTS, EXPERTS])
        equal = sb("equal", [P, TILES, EXPERTS, EXPERTS])
        rank8 = sb("rank8", [P, TILES, EXPERTS])
        gate = sb("gate", [P, TILES, EXPERTS])
        gate_rows = sb("gate_rows", [EXPERTS, T])
        gate_b = sb("gate_b", [P, EXPERTS, T])
        xe = sb("xe", [P, 2, T])
        tanh_g = sb("tanh_g", [P, T])
        gated = sb("gated", [P, T])
        hid = sb("hid", [P, 2, T])
        z2 = sb("z2", [P, TILES, C])
        stats2 = sb("stats2", [P, TILES, 6])
        mv2 = sb("mv2", [P, TILES, 2])
        rstd2 = sb("rstd2", [P, TILES])
        y_sb = sb("y_sb", [P, 2, TILES, C])

        bank_a = bank("bank_a")
        bank_b = bank("bank_b")
        bank_kv = bank("bank_kv")
        bank_o = bank("bank_o")
        bank_m = bank("bank_m")
        bank_g = bank("bank_g")
        bank_u = bank("bank_u")
        bank_f = bank("bank_f")

        weights_in = sem("weights_in")
        xt_in = [sem("xt_in0"), sem("xt_in1")]
        xn_in = [sem("xn_in0"), sem("xn_in1")]
        qbd_in = [sem("qbd_in0"), sem("qbd_in1")]
        gate_out = sem("gate_out")
        gate_in = sem("gate_in")
        y_out = [sem("y_out0"), sem("y_out1")]
        tables_ready = sem("tables_ready")
        zeroed = sem("zeroed")
        half_set = sem("half_set")
        ones_zeroed = sem("ones_zeroed")
        q_done = sem("q_done")
        kv_done = sem("kv_done")
        tp_done = sem("tp_done")
        count_done = sem("count_done")
        a_done = sem("a_done")
        b_done = sem("b_done")
        o_done = sem("o_done")
        y_done = sem("y_done")
        x1t_done = sem("x1t_done")
        logit_done = sem("logit_done")
        gatet_done = sem("gatet_done")
        g_done = sem("g_done")
        u_done = sem("u_done")
        ffn_done = sem("ffn_done")
        q_ready = sem("q_ready")
        vals_ready = sem("vals_ready")
        kt_ready = sem("kt_ready")
        exp_done = sem("exp_done")
        x1t_ready = sem("x1t_ready")
        lexp_ready = sem("lexp_ready")
        gate_rows_ready = sem("gate_rows_ready")
        tanh_done = sem("tanh_done")
        kvs_ready = sem("kvs_ready")
        ties_done = sem("ties_done")
        beats_ready = sem("beats_ready")
        perm_ready = sem("perm_ready")
        mask_ready = sem("mask_ready")
        max_ready = sem("max_ready")
        weighted = sem("weighted")
        rden_done = sem("rden_done")
        attn_ready = sem("attn_ready")
        z1_ready = sem("z1_ready")
        stats_done = sem("stats_done")
        mv_ready = sem("mv_ready")
        x1_ready = sem("x1_ready")
        gate_step = sem("gate_step")
        lsub_ready = sem("lsub_ready")
        gate_ready = sem("gate_ready")
        xe_ready = sem("xe_ready")
        gated_done = sem("gated_done")
        hid_ready = sem("hid_ready")
        z2_ready = sem("z2_ready")
        stats2_done = sem("stats2_done")
        mv2_ready = sem("mv2_ready")
        waited = sem("waited")
        y_ready = sem("y_ready")
        res_ready = sem("res_ready")
        var_done = sem("var_done")
        rstd_ready = sem("rstd_ready")
        var2_done = sem("var2_done")
        rstd2_ready = sem("rstd2_ready")

        N_WEIGHTS = 12
        N_MASKED = 2 * NBLK
        PART = NBLK // 2
        QBD_DMAS = 2 * HEADS

        def wait(eng, s, count):
            if not (isinstance(count, int) and count <= 0):
                eng.wait_ge(s, count)

        class Seq:

            def __init__(self, n, half, d=0):
                self.n, self.half = n + (half + d) // 2, (half + d) % 2
                self.b = 2 * self.n + self.half

        LOOP_FROM, LOOP_TO = 2, B - 2

        def steps(eng, step):
            def peeled(b):
                step(b // 2, b % 2, lambda d: 0 <= b + d < B)

            for b in range(LOOP_FROM):
                peeled(b)
            with eng.Fori(0, (LOOP_TO - LOOP_FROM) // 2) as i:
                for half in range(2):
                    step(i + LOOP_FROM // 2, half, lambda d: True)
            for b in range(LOOP_TO, B + 2):
                peeled(b)

        block = ctx.enter_context(nc.Block())

        @block.sync
        def _(sp):
            loads = [(table[:], consts), (wq_sb[:], wq_t), (bq_sb[:], bq), (wkvs_sb[:], w_kvs),
                     (bias_all[:], b_kvs.to_broadcast([P, KVS])),
                     (bias_new[KEEP:P, :], b_kvs.to_broadcast([P - KEEP, KVS])),
                     (wo_sb[:], wo_t), (bo_sb[:], bo.to_broadcast([P, C])), (gate_w[:], gate_t),
                     (w1_sb[:], w1), (w3_sb[:], w3), (w2_sb[:], w2)]

            def load_xt(s):
                sp.dma_start(xt_sb[:, s.half, :], x_t[s.b]).then_inc(xt_in[s.half], 16)

            def load_xn(s):
                sp.dma_start(xn_sb[:, s.half, :, :],
                             x[s.b].rearrange("(t p) c -> p t c", p=P)).then_inc(xn_in[s.half], 16)

            def hold(s, count):
                wait(sp, s, count)
                sp.sem_inc(waited, 1)

            def spread_queries(s, part):
                blocks = slice(part * PART, (part + 1) * PART)
                for src, dst in ((q_sb, qbd), (qb_sb, qbd_bf)):
                    for h in range(HEADS):
                        rows = slice(h * HS, (h + 1) * HS)
                        sp.dma_start(dst[rows, blocks, h, :],
                                     src[rows, s.half, :].rearrange("p (k q) -> p k q", q=QB)[:, blocks, :]
                                     ).then_inc(qbd_in[part], 16)

            load_xt(Seq(0, 0))
            for dst, src in loads:
                sp.dma_start(dst, src).then_inc(weights_in, 16)
            load_xn(Seq(0, 0))
            sp.wait_ge(zeroed, 2)
            sp.wait_ge(q_ready, 1)
            spread_queries(Seq(0, 0), 0)

            def step(n, half, has):
                now, nxt, prev, prev2 = Seq(n, half), Seq(n, half, 1), Seq(n, half, -1), Seq(n, half, -2)
                if has(0):
                    hold(b_done, N_MASKED * now.b)
                    spread_queries(now, 1)
                if has(1):
                    hold(kv_done, NCAND * now.b)
                    load_xt(nxt)
                    hold(z1_ready, TILES * now.b)
                    load_xn(nxt)
                    hold(q_ready, nxt.b + 1)
                    hold(b_done, N_MASKED * now.b + NBLK)
                    spread_queries(nxt, 0)
                if has(-1):
                    hold(gate_rows_ready, prev.b + 1)
                    sp.dma_start(gate_dram[prev.half], gate_rows[:]).then_inc(gate_out, 16)
                    hold(gate_out, 16 * prev.b + 16)
                    hold(xe_ready, EXPERTS * prev.b)
                    sp.dma_start(gate_b[:].rearrange("p e t -> p (e t)"),
                                 gate_dram[prev.half].rearrange("e t -> (e t)").partition_broadcast(P)
                                 ).then_inc(gate_in, 16)
                if has(-2):
                    hold(y_ready, prev2.b + 1)
                    sp.dma_start(out[prev2.b].rearrange("(t p) c -> p t c", p=P),
                                 y_sb[:, prev2.half, :, :]).then_inc(y_out[prev2.half], 16)

            steps(sp, step)
            for half in range(2):
                sp.wait_ge(y_out[half], 16 * (B // 2))

        @block.gpsimd
        def _(pool):
            pool.memset(qbd[:], 0.0).then_inc(zeroed, 1)
            pool.memset(minus_half[:], -0.5).then_inc(half_set, 1)
            pool.memset(eps[:], EPS).then_inc(half_set, 1)
            pool.wait_ge(half_set, 2)
            pool.wait_ge(weights_in, 16 * N_WEIGHTS)

            def step(n, half, has):
                now, prev, prev2 = Seq(n, half), Seq(n, half, -1), Seq(n, half, -2)
                if has(0):
                    pool.wait_ge(xn_in[now.half], 16 * now.n + 16)
                    pool.tensor_tensor(xn_sb[:, now.half], xn_sb[:, now.half],
                                       bo_sb[:].unsqueeze(1).to_broadcast([P, TILES, C]),
                                       ALU.add).then_inc(res_ready, 1)
                if has(-1):
                    pool.wait_ge(mv_ready, prev.b + 1)
                    pool.tensor_tensor(var[:], mv[:, :, 1], eps[:], ALU.add).then_inc(var_done, 1)
                    pool.wait_ge(var_done, prev.b + 1)
                    pool.tensor_tensor(rstd[:], var[:], minus_half[:], ALU.pow).then_inc(rstd_ready, 1)
                if has(-2):
                    pool.wait_ge(mv2_ready, prev2.b + 1)
                    pool.tensor_tensor(var2[:], mv2[:, :, 1], eps[:], ALU.add).then_inc(var2_done, 1)
                    pool.wait_ge(var2_done, prev2.b + 1)
                    pool.tensor_tensor(rstd2[:], var2[:], minus_half[:], ALU.pow).then_inc(rstd2_ready, 1)

            steps(pool, step)

        @block.tensor
        def _(pe):
            def mm(out_, lhs, rhs, start=True, stop=True):
                return pe.matmul(out_, lhs, rhs, start=start, stop=stop, skip_group_check=True)

            m_reader = [None]

            def use_bank_m(reader, count_after):
                if m_reader[0]:
                    pe.wait_ge(*m_reader[0])
                m_reader[0] = (reader, count_after)

            def queries(s):
                pe.wait_ge(xt_in[s.half], 16 * s.n + 16)
                use_bank_m(q_ready, s.b + 1)
                mm(bank_m[:], wq_sb[:], xt_sb[:, s.half, :]).then_inc(q_done, 1)

            def project(s, c):
                wait(pe, mask_ready, NCAND * s.b + c - 1)
                if c == 1:
                    mm(bank_kv[:, 0:KVS], xt_sb[:, s.half, 0:P], wkvs_sb[:]).then_inc(kv_done, 1)
                    return
                mm(bank_kv[KEEP:P, 0:KVS], xt_sb[:, s.half, QB * c:QB * (c + 1)], wkvs_sb[:])
                pe.wait_ge(perm_ready, (NCAND - 1) * s.b + c - 1)
                mm(bank_kv[0:KEEP, 0:KVS], perm[:], kvs[:, c - 2, :]).then_inc(kv_done, 1)

            def turn(s, c):
                pe.wait_ge(kvs_ready, NCAND * s.b + c)
                pe.transpose(bank_kv[:, 3 * P:4 * P], kvs[:, c - 1, 2 * C:KVS].to_broadcast([P, P]), ident)
                use_bank_m(kt_ready, NCAND * s.b + c)
                pe.transpose(bank_m[:, 0:P], kvs[:, c - 1, 0:C], ident).then_inc(tp_done, 1)

            def count(s, c):
                pe.wait_ge(beats_ready, NCAND * s.b + c)
                mm(bank_kv[:, 3 * P:4 * P], seen_bf[:], beats[:], stop=False)
                mm(bank_kv[:, 3 * P:4 * P], ident_bf[:], future_bf[:], start=False).then_inc(count_done, 1)

            def logits_a(s, k, g):
                c = max(k, 1) - 1
                if k % PART == 0 and g == 0:
                    pe.wait_ge(qbd_in[k // PART], QBD_DMAS * 16 * (s.b + 1))
                if k == 0 and g == 0:
                    pe.wait_ge(kt_ready, NCAND * s.b + 1)
                if k > 0 and g == 0:
                    pe.wait_ge(mask_ready, NCAND * s.b + k)
                    pe.wait_ge(kt_ready, NCAND * s.b + k)
                wait(pe, max_ready, N_MASKED * s.b + 2 * k + g)
                mm(bank_a[:], ident_bf[:], mask[:, k, :].unsqueeze(1).to_broadcast([P, 4, P]), stop=False)
                for p in range(4):
                    last = mm(bank_a[:, p * P:(p + 1) * P],
                              qbd_bf[:, k, 8 * g + 2 * p:8 * g + 2 * p + 2, :].rearrange("p h q -> p (h q)"),
                              kt_bf[:, c, :], start=False, stop=p == 3)
                last.then_inc(a_done, 1)

            def logits_b(s, k, g):
                c = max(k, 1) - 1
                wait(pe, exp_done, N_MASKED * s.b + 2 * k + g)
                mm(bank_b[:], kt[:, c, :], qbd[:, k, 8 * g:8 * g + 8, :].rearrange("p h q -> p (h q)"),
                   stop=False)
                mm(bank_b[:], mask[:, k, :], ident_bf[:].unsqueeze(1).to_broadcast([P, 4, P]),
                   start=False, stop=False)
                pe.wait_ge(max_ready, N_MASKED * s.b + 2 * k + g + 1)
                for p in range(4):
                    last = mm(bank_b[:, p * P:(p + 1) * P],
                              rowmax[:, k % 2, 4 * g + p:4 * g + p + 1].to_broadcast([P, P]),
                              negid_bf[:], start=False, stop=p == 3)
                last.then_inc(b_done, 1)

            def values(s, k):
                c = max(k, 1) - 1
                wait(pe, attn_ready, NBLK * s.b + k)
                pe.wait_ge(vals_ready, NCAND * s.b + c + 1)
                pe.wait_ge(exp_done, N_MASKED * s.b + 2 * k + 2)
                if k == 0:
                    pe.wait_ge(weighted, s.b + 1)
                for col in range(2):
                    for pair in range(2):
                        for g in range(GRP):
                            rows = slice(32 * g, 32 * g + 32)
                            lhs = ones_pair[:, pair, :] if col else vals[:, c, pair, rows]
                            h = 4 * g + 2 * pair
                            last = mm(bank_o[rows, P * col:P * (col + 1)], lhs,
                                      probs[:, k % 2, h:h + 2, :].rearrange("p h q -> p (h q)"),
                                      start=col == 0 and pair == 0, stop=pair == 1)
                last.then_inc(o_done, 1)

            def project_out(s, j):
                pe.wait_ge(attn_ready, NBLK * s.b + 2 * j + 2)
                use_bank_m(z1_ready, TILES * s.b + j + 1)
                for h in range(2):
                    last = mm(bank_m[:, 0:C], attn[:, h].rearrange("p k q -> p (k q)"), wo2[:, h, :],
                              start=h == 0, stop=h == 1)
                last.then_inc(y_done, 1)

            def turn_x1(s):
                pe.wait_ge(x1_ready, s.b + 1)
                use_bank_m(x1t_ready, s.b + 1)
                for t in range(TILES):
                    last = pe.transpose(bank_m[:, t * P:(t + 1) * P], x1[:, s.half, t, :], ident)
                last.then_inc(x1t_done, 1)

            def gate_logits(s):
                pe.wait_ge(x1t_ready, s.b + 1)
                use_bank_m(lsub_ready, s.b + 1)
                for t in range(TILES):
                    last = mm(bank_m[:, EXPERTS * t:EXPERTS * (t + 1)], x1t[:, s.half, t * P:(t + 1) * P], gate_w[:])
                last.then_inc(logit_done, 1)

            def turn_gates(s):
                pe.wait_ge(gate_ready, s.b + 1)
                use_bank_m(gate_rows_ready, s.b + 1)
                for t in range(TILES):
                    last = pe.transpose(bank_m[0:EXPERTS, t * P:(t + 1) * P], gate[:, t, :], ident)
                last.then_inc(gatet_done, 1)

            def up(s, n):
                e = ORDER[n]
                wait(pe, hid_ready, NE * s.b + n)
                if n > 0:
                    pe.wait_ge(xe_ready, EXPERTS * s.b + n)
                src = x1t[:, s.half, :] if n == 0 else xe[:, n % 2, :]
                mm(bank_g[:], w1_sb[:, e, :], src).then_inc(g_done, 1)
                mm(bank_u[:], w3_sb[:, e, :], src).then_inc(u_done, 1)

            def down(s, n):
                e = ORDER[n]
                pe.wait_ge(hid_ready, NE * s.b + n + 1)
                if n == 0:
                    wait(pe, z2_ready, s.b)
                for t in range(TILES):
                    last = mm(bank_f[:, t * C:(t + 1) * C], hid[:, (s.half + n) % 2, t * P:(t + 1) * P], w2_sb[:, e, :],
                              start=n == 0 and t == 0, stop=n == NE - 1)
                if n == NE - 1:
                    last.then_inc(ffn_done, 1)

            pe.wait_ge(weights_in, 16 * N_WEIGHTS)
            pe.wait_ge(tables_ready, 1)
            queries(Seq(0, 0))
            project(Seq(0, 0), 1)
            turn(Seq(0, 0), 1)

            def step(n, half, has):
                now, nxt, prev, prev2 = Seq(n, half), Seq(n, half, 1), Seq(n, half, -1), Seq(n, half, -2)
                if has(0):
                    m_reader[0] = (kt_ready, NCAND * now.b + 1)
                for k in range(NBLK):
                    if has(0):
                        logits_a(now, k, 0)
                    if k < 6 and has(-2):
                        up(prev2, k + 2)
                    if k >= 6 and has(-1):
                        up(prev, k - 6)
                    if has(0):
                        logits_a(now, k, 1)
                    if k == 4 and has(-1):
                        turn_x1(prev)
                    if has(0) and k > 0:
                        logits_b(now, k - 1, 0)
                    if has(-1) and k == 0:
                        logits_b(prev, NBLK - 1, 0)
                    if has(0) and k < NCAND:
                        count(now, k + 1)
                    if k < 6 and has(-2):
                        down(prev2, k + 1)
                    if k == 6 and has(-2):
                        down(prev2, 8)
                    if k == 7 and has(-1):
                        down(prev, 0)
                    if has(0) and k > 0:
                        logits_b(now, k - 1, 1)
                    if has(-1) and k == 0:
                        logits_b(prev, NBLK - 1, 1)
                    if has(0) and k + 2 <= NCAND:
                        project(now, k + 2)
                    if has(1) and k == NBLK - 1:
                        project(nxt, 1)
                    if k in (4, 6) and has(0):
                        project_out(now, k // 2 - 2)
                    if k in (0, 2) and has(-1):
                        project_out(prev, k // 2 + 2)
                    if k >= 2 and has(0):
                        values(now, k - 2)
                    if k < 2 and has(-1):
                        values(prev, NBLK - 2 + k)
                    if has(0) and k + 2 <= NCAND:
                        turn(now, k + 2)
                    if has(1) and k == NBLK - 1:
                        turn(nxt, 1)
                    if k == 3 and has(1):
                        queries(nxt)
                    if k == 4 and has(-1):
                        gate_logits(prev)
                    if k == 5 and has(-2):
                        up(prev2, 8)
                        down(prev2, 7)
                    if k == 5 and has(-1):
                        turn_gates(prev)

            steps(pe, step)

        @block.scalar
        def _(act):
            act.wait_ge(weights_in, 16 * N_WEIGHTS)

            def queries(s):
                act.wait_ge(q_done, s.b + 1)
                act.activation(q_sb[:, s.half, :], bank_m[:], ACT.Identity, bias=bq_sb[:])
                act.activation(qb_sb[:, s.half, :], bank_m[:], ACT.Identity, bias=bq_sb[:]).then_inc(q_ready, 1)

            def pair_values(s, c):
                act.wait_ge(kvs_ready, NCAND * s.b + c)
                for pair in range(2):
                    last = act.activation(
                        vals[:, c - 1, pair].rearrange("p (g r i) -> p g r i", g=GRP, r=2)[:, :, pair, :],
                        kvs[:, c - 1, C:2 * C].rearrange("p (g r i) -> p g r i", g=GRP, r=2)[:, :, pair, :], ACT.Copy)
                last.then_inc(vals_ready, 1)

            def keys(s, c):
                act.wait_ge(tp_done, NCAND * s.b + c)
                act.activation(kt_bf[:, c - 1, :], bank_m[:, 0:P], ACT.Copy)
                act.activation(kt[:, c - 1, :], bank_m[:, 0:P], ACT.Copy).then_inc(kt_ready, 1)

            def exps(s, k, g):
                act.wait_ge(b_done, N_MASKED * s.b + 2 * k + g + 1)
                act.activation(probs[:, k % 2, 8 * g:8 * g + 8, :].rearrange("p h q -> p (h q)"),
                               bank_b[:], ACT.Exp, scale=SCALE).then_inc(exp_done, 1)

            def tanh(s, n):
                act.wait_ge(g_done, NE * s.b + n + 1)
                act.activation(tanh_g[:], bank_g[:], ACT.Tanh, scale=0.5).then_inc(tanh_done, 1)

            queries(Seq(0, 0))
            pair_values(Seq(0, 0), 1)
            keys(Seq(0, 0), 1)

            def step(n, half, has):
                now, nxt, prev, prev2 = Seq(n, half), Seq(n, half, 1), Seq(n, half, -1), Seq(n, half, -2)
                for k in range(NBLK):
                    if k < 6 and has(-2):
                        tanh(prev2, k + 2)
                    if k >= 6 and has(-1):
                        tanh(prev, k - 6)
                    if k == 4 and has(-1):
                        act.wait_ge(x1t_done, prev.b + 1)
                        act.activation(x1t[:, prev.half, :], bank_m[:], ACT.Copy).then_inc(x1t_ready, 1)
                    for g in range(2):
                        if has(0) and k > 0:
                            exps(now, k - 1, g)
                        if has(-1) and k == 0:
                            exps(prev, NBLK - 1, g)
                        if k == 5 and g == 0 and has(-1):
                            act.wait_ge(lsub_ready, prev.b + 1)
                            act.activation(lexp[:], lsub[:], ACT.Exp).then_inc(lexp_ready, 1)
                    if has(0) and k + 2 <= NCAND:
                        pair_values(now, k + 2)
                        keys(now, k + 2)
                    if has(1) and k == NBLK - 1:
                        pair_values(nxt, 1)
                        keys(nxt, 1)
                    if k == 3 and has(1):
                        queries(nxt)
                    if k == 5 and has(-2):
                        tanh(prev2, 8)
                    if k == 5 and has(-1):
                        act.wait_ge(gatet_done, prev.b + 1)
                        act.activation(gate_rows[:], bank_m[0:EXPERTS, :], ACT.Copy).then_inc(gate_rows_ready, 1)

            steps(act, step)

        @block.vector
        def _(dve):
            dve.memset(qbd_bf[:], 0.0).then_inc(zeroed, 1)
            dve.memset(vals[:], 0.0)
            dve.memset(ones_pair[:], 0.0).then_inc(ones_zeroed, 1)
            dve.memset(bias_new[0:KEEP, :], 0.0)
            dve.wait_ge(ones_zeroed, 1)
            for pair in range(2):
                dve.memset(ones_pair[:, pair, 16 * pair:16 * pair + 16], 1.0)
            dve.wait_ge(weights_in, 16 * N_WEIGHTS)
            dve.tensor_copy(ident_bf[:], ident)
            dve.tensor_scalar(negid_bf[:], ident, -1.0, None, ALU.mult)
            dve.tensor_copy(seen_bf[:], tables["seen"])
            dve.tensor_copy(future_bf[:], tables["future"])
            dve.tensor_scalar(mask[:, 0, :], tables["future0"], MASKED, None, ALU.mult)
            for h in range(2):
                last = dve.tensor_scalar(wo2[:, h, :], wo_sb[:], tables["odd"][:, h:h + 1], None, ALU.mult)
            last.then_inc(tables_ready, 1)

            def candidates(s, c):
                dve.wait_ge(kv_done, NCAND * s.b + c)
                bias = bias_all if c == 1 else bias_new
                dve.tensor_tensor(kvs[:, c - 1, :], bank_kv[:, 0:KVS], bias[:], ALU.add).then_inc(kvs_ready, 1)

            def ranks(s, c):
                dve.wait_ge(tp_done, NCAND * s.b + c)
                own = kvs[:, c - 1, 2 * C:KVS]
                dve.scalar_tensor_tensor(ties[:], bank_kv[:, 3 * P:4 * P], own, tables["before"],
                                         ALU.is_equal, ALU.mult).then_inc(ties_done, 1)
                dve.wait_ge(ties_done, NCAND * s.b + c)
                dve.scalar_tensor_tensor(beats[:], bank_kv[:, 3 * P:4 * P], own, ties[:],
                                         ALU.is_lt, ALU.add, accum_out=wins[:]).then_inc(beats_ready, 1)
                if c < NCAND:
                    dve.wait_ge(beats_ready, NCAND * s.b + c)
                    dve.tensor_scalar(perm[:], tables["slot"], wins[:], None, ALU.is_equal).then_inc(perm_ready, 1)

            def masks(s, c):
                dve.wait_ge(count_done, NCAND * s.b + c)
                dve.tensor_scalar(mask[:, c, :], bank_kv[:, 3 * P:4 * P], KEEP - 0.5, MASKED,
                                  ALU.is_ge, ALU.mult).then_inc(mask_ready, 1)

            def maxima(s, k, g):
                dve.wait_ge(a_done, N_MASKED * s.b + 2 * k + g + 1)
                dve.tensor_reduce(rowmax[:, k % 2, 4 * g:4 * g + 4],
                                  bank_a[:].rearrange("p (a j) -> p a j", a=4), AX_X, ALU.max).then_inc(max_ready, 1)

            def weigh(s):
                dve.wait_ge(exp_done, N_MASKED * s.b + 2)
                e = probs[0:QB, 0, :, :]
                dve.tensor_tensor(e, e, tables["times"][0:QB, :].unsqueeze(1).to_broadcast([QB, HEADS, QB]),
                                  ALU.mult).then_inc(weighted, 1)

            def normalise(s, k):
                dve.wait_ge(o_done, NBLK * s.b + k + 1)
                dve.reciprocal(rden[:].rearrange("p h q -> p (h q)"), bank_o[:, P:2 * P]).then_inc(rden_done, 1)
                dve.wait_ge(rden_done, NBLK * s.b + k + 1)
                dve.tensor_tensor(attn[:, :, k % 2, :], bank_o[:, 0:P].rearrange("p (h q) -> p h q", h=2),
                                  rden[:], ALU.mult).then_inc(attn_ready, 1)

            def residual(s, j):
                dve.wait_ge(y_done, TILES * s.b + j + 1)
                if j == 0:
                    dve.wait_ge(res_ready, s.b + 1)
                dve.tensor_tensor(z1[:, j, :], bank_m[:, 0:C], xn_sb[:, s.half, j, :], ALU.add).then_inc(z1_ready, 1)

            def layernorm_stats(s, z, z_sem, z_count, st, st_sem, mv_, mv_sem):
                dve.wait_ge(z_sem, z_count)
                for t in range(TILES):
                    dve.bn_stats(st[:, t, :], z[:, t, :]).then_inc(st_sem, 1)
                dve.wait_ge(st_sem, TILES * s.b + TILES)
                dve.sem_inc(waited, 1)
                for t in range(TILES):
                    last = dve.bn_aggr(mv_[:, t, :], st[:, t, :])
                last.then_inc(mv_sem, 1)

            def layernorm_apply(s, z, mv_, rstd_, rstd_sem, dst, dst_sem):
                dve.wait_ge(rstd_sem, s.b + 1)
                for t in range(TILES):
                    last = dve.tensor_scalar(dst[:, s.half, t, :], z[:, t, :], mv_[:, t, 0:1], rstd_[:, t:t + 1],
                                             ALU.subtract, ALU.mult)
                last.then_inc(dst_sem, 1)

            over_e = [P, TILES, EXPERTS]
            over_ee = [P, TILES, EXPERTS, EXPERTS]

            def gates_shift(s):
                logits = bank_m[:, 0:TILES * EXPERTS].rearrange("p (t e) -> p t e", e=EXPERTS)
                dve.wait_ge(logit_done, s.b + 1)
                dve.tensor_reduce(lmax[:], logits, AX_X, ALU.max).then_inc(gate_step, 1)
                dve.wait_ge(gate_step, 9 * s.b + 1)
                dve.tensor_tensor(lsub[:], logits, lmax[:].unsqueeze(2).to_broadcast(over_e),
                                  ALU.subtract).then_inc(lsub_ready, 1)

            def gates(s):
                at = [1]

                def step_of(ins):
                    at[0] += 1
                    ins.then_inc(gate_step, 1)
                    dve.wait_ge(gate_step, 9 * s.b + at[0])

                dve.wait_ge(lexp_ready, s.b + 1)
                step_of(dve.tensor_reduce(lsum[:], lexp[:], AX_X, ALU.add))
                step_of(dve.reciprocal(linv[:], lsum[:]))
                step_of(dve.tensor_tensor(score[:], lexp[:], linv[:].unsqueeze(2).to_broadcast(over_e), ALU.mult))
                other = score[:].unsqueeze(2).to_broadcast(over_ee)
                own = score[:].unsqueeze(3).to_broadcast(over_ee)
                step_of(dve.tensor_tensor(equal[:], other, own, ALU.is_equal))
                step_of(dve.tensor_tensor(equal[:].rearrange("p t e f -> p t (e f)"),
                                          equal[:].rearrange("p t e f -> p t (e f)"),
                                          tables["lower8"].unsqueeze(1).to_broadcast([P, TILES, EXPERTS ** 2]),
                                          ALU.mult))
                step_of(dve.tensor_tensor(better[:], other, own, ALU.is_gt))
                step_of(dve.tensor_tensor(better[:], better[:], equal[:], ALU.add))
                step_of(dve.tensor_reduce(rank8[:], better[:], AX_X, ALU.add))
                dve.scalar_tensor_tensor(gate[:], rank8[:], 1.5, score[:], ALU.is_lt, ALU.mult).then_inc(gate_ready, 1)

            def scale_x(s, n):
                if n == 1:
                    dve.wait_ge(gate_in, 16 * s.b + 16)
                dve.tensor_tensor(xe[:, n % 2, :], x1t[:, s.half, :], gate_b[:, ORDER[n], :],
                                  ALU.mult).then_inc(xe_ready, 1)

            def hidden(s, n):
                dve.wait_ge(tanh_done, NE * s.b + n + 1)
                dve.scalar_tensor_tensor(gated[:], tanh_g[:], 1.0, bank_g[:],
                                         ALU.add, ALU.mult).then_inc(gated_done, 1)
                dve.wait_ge(u_done, NE * s.b + n + 1)
                dve.wait_ge(gated_done, NE * s.b + n + 1)
                dve.scalar_tensor_tensor(hid[:, (s.half + n) % 2, :], gated[:], 0.5, bank_u[:],
                                         ALU.mult, ALU.mult).then_inc(hid_ready, 1)

            candidates(Seq(0, 0), 1)
            ranks(Seq(0, 0), 1)

            def step(n, half, has):
                now, nxt, prev, prev2 = Seq(n, half), Seq(n, half, 1), Seq(n, half, -1), Seq(n, half, -2)
                for k in range(NBLK):
                    if k == 5 and has(-1):
                        gates_shift(prev)
                    if has(0):
                        maxima(now, k, 0)
                    if k == 6 and has(-2):
                        hidden(prev2, 8)
                    if k == 7 and has(-1):
                        scale_x(prev, 1)
                    if k < 6 and has(-2):
                        scale_x(prev2, k + 3)
                    if has(0):
                        maxima(now, k, 1)
                    if k == 3 and has(-1):
                        layernorm_apply(prev, z1, mv, rstd, rstd_ready, x1, x1_ready)
                    if k == 7 and has(-2):
                        layernorm_apply(prev2, z2, mv2, rstd2, rstd2_ready, y_sb, y_ready)
                    if k < 6 and has(-2):
                        hidden(prev2, k + 2)
                    if has(0) and k < NCAND:
                        masks(now, k + 1)
                    if k >= 6 and has(-1):
                        hidden(prev, k - 6)
                    if k == 7 and has(-1):
                        scale_x(prev, 2)
                    if k == 1 and has(0):
                        weigh(now)
                    if k == 5 and has(-1):
                        gates(prev)
                    if has(0) and k + 2 <= NCAND:
                        candidates(now, k + 2)
                    if has(1) and k == NBLK - 1:
                        candidates(nxt, 1)
                    if k in (4, 6) and has(0):
                        residual(now, k // 2 - 2)
                    if k in (0, 2) and has(-1):
                        residual(prev, k // 2 + 2)
                    if k >= 2 and has(0):
                        normalise(now, k - 2)
                    if k < 2 and has(-1):
                        normalise(prev, NBLK - 2 + k)
                    if has(0) and k + 2 <= NCAND:
                        ranks(now, k + 2)
                    if has(1) and k == NBLK - 1:
                        ranks(nxt, 1)
                    if k == 2 and has(-1):
                        layernorm_stats(prev, z1, z1_ready, TILES * prev.b + TILES, stats, stats_done, mv, mv_ready)
                    if k == 6 and has(-2):
                        dve.wait_ge(ffn_done, prev2.b + 1)
                        dve.tensor_tensor(z2[:], bank_f[:].rearrange("p (t c) -> p t c", c=C), x1[:, prev2.half],
                                          ALU.add).then_inc(z2_ready, 1)
                        layernorm_stats(prev2, z2, z2_ready, prev2.b + 1, stats2, stats2_done, mv2, mv2_ready)

            steps(dve, step)


def kernel(**inputs):
    import concourse.bacc as bacc
    from concourse.bass_utils import run_bass_kernel_spmd

    a = {k.replace("L0_", ""): np.asarray(v) for k, v in inputs.items()}
    experts = {n: np.concatenate([a[f"ffn_{n}"], a[f"ffn_{n}s"]]) for n in ("w1", "w3", "w2")}
    arrays = {
        "x": a["attn_x"],
        "x_t": a["attn_x"].transpose(0, 2, 1),
        "wq_t": a["attn_Wq"].T,
        "bq": a["attn_bq"][:, None],
        "w_kvs": np.concatenate([a["attn_Wk"].T, a["attn_Wv"].T, a["attn_Wks"][:, None]], axis=1),
        "b_kvs": np.concatenate([a["attn_bk"], a["attn_bv"], a["attn_bks"].reshape(1)])[None, :],
        "wo_t": a["attn_Wo"].T,
        "bo": a["attn_bo"][None, :],
        "gate_t": a["ffn_gate_w"].T,
        "w1": experts["w1"].transpose(1, 0, 2),
        "w3": experts["w3"].transpose(1, 0, 2),
        "w2": experts["w2"].transpose(1, 0, 2),
        "consts": shape_constants(),
    }
    nc = bacc.Bacc("TRN2", target_bir_lowering=False, num_devices=1)
    arrays = {f"in_{n}": np.ascontiguousarray(v) for n, v in arrays.items()}
    args = [nc.dram_tensor(n, v.shape, mybir.dt.from_np(v.dtype), kind="ExternalInput").ap() for n, v in arrays.items()]
    args.append(nc.dram_tensor("out_y", (B, T, C), F32, kind="ExternalOutput").ap())
    post_ln_layer(nc, *args)
    r = run_bass_kernel_spmd(nc, [arrays], core_ids=[0])
    return r.results[0]["out_y"]
```

```python
from contextlib import ExitStack

import numpy as np

import concourse.bass as bass
from concourse import mybir

ALU = mybir.AluOpType
ACT = mybir.ActivationFunctionType
F32 = mybir.dt.float32
BF16 = mybir.dt.bfloat16
F32R = mybir.dt.float32r
AX_X = mybir.AxisListType.X

P = 128
B, T, C = 16, 512, 128
HEADS = 16
HS = C // HEADS
KEEP = 64
QB = 64
NBLK = T // QB
NCAND = NBLK - 1
EXPERTS = 8
NE = EXPERTS + 1
HIDDEN = 128
TILES = T // P
SCALE = 1.0 / HS ** 0.5
EPS = 1e-5
MASKED = -1e30
KVS = 2 * C + 1
PAIRS = HEADS // 2
GRP = 4
SHARED = EXPERTS
ORDER = [SHARED] + list(range(EXPERTS))

FIRST_PARTS = [("seen", P), ("future", P), ("future0", P)]
CONST_PARTS = [("ident", P), ("before", P),
               ("slot", KEEP), ("times", QB), ("lower8", EXPERTS * EXPERTS), ("odd", 2),
               ("head", HEADS)]


def shape_constants():
    r = np.arange(P)[:, None]
    c = np.arange(P)[None, :]
    u = r % QB
    t = {
        "ident": (r == c),
        "seen": (r < KEEP) | (r - KEEP <= c % QB),
        "future": KEEP * (c - KEEP > u),
        "future0": (c > u),
        "before": (r < c),
        "slot": np.broadcast_to(P - 1 - np.arange(KEEP), (P, KEEP)),
        "times": np.where(np.arange(QB)[None, :] == r, KEEP - np.arange(QB)[None, :], 1),
        "lower8": np.broadcast_to(np.tril(np.ones((EXPERTS, EXPERTS)), -1).reshape(1, -1), (P, EXPERTS ** 2)),
        "head": (r // HS == np.arange(HEADS)[None, :]),
        "odd": (np.arange(P)[:, None] // HS % 2 == np.arange(2)[None, :]),
    }
    return [np.concatenate([np.asarray(t[n], np.float32).reshape(P, w) for n, w in parts], axis=1)
            for parts in (CONST_PARTS, FIRST_PARTS)]


def post_ln_layer(nc, x, x_t, wq_t, bq, w_kvs, b_kvs, wo_t, bo, gate_t, w1, w3, w2, consts, first_consts, out):
    gate_dram = nc.dram_tensor("gate_dram", (2, EXPERTS, T), F32, kind="Internal").ap()
    with ExitStack() as ctx:
        def sb(name, shape, dt=F32):
            return ctx.enter_context(nc.sbuf_tensor(name, shape, dt))

        def bank(name):
            return ctx.enter_context(nc.psum_tensor(name, [P, 512], F32))

        def sem(name):
            return ctx.enter_context(nc.semaphore(name))

        n_const = sum(w for _, w in CONST_PARTS)
        table = sb("table", [P, n_const])
        at, tables = 0, {}
        for n, w in CONST_PARTS:
            tables[n] = table[:, at:at + w]
            at += w
        ident = tables["ident"]
        ident_bf = sb("ident_bf", [P, P], BF16)
        negid_bf = sb("negid_bf", [P, P], BF16)
        seen_bf = sb("seen_bf", [P, P], BF16)
        future_bf = sb("future_bf", [P, P], BF16)
        ones_pair = sb("ones_pair", [P, 2, 32])
        wq_sb = sb("wq_sb", [P, C])
        bq_sb = sb("bq_sb", [P, 1])
        wkvs_sb = sb("wkvs_sb", [P, KVS])
        bias_all = sb("bias_all", [P, KVS])
        bias_new = sb("bias_new", [P, KVS])
        wo2 = sb("wo2", [P, 2, C])
        bo_sb = sb("bo_sb", [P, C])
        gate_w = sb("gate_w", [P, EXPERTS])
        w_hi = sb("w_hi", [P, 2, NE, HIDDEN], F32R)
        w_lo = sb("w_lo", [P, 2, NE, HIDDEN], F32R)
        w2_sb = sb("w2_sb", [P, NE, C])
        xt_sb = sb("xt_sb", [P, 2, T])
        xn_sb = sb("xn_sb", [P, 2, TILES, C])
        q_sb = sb("q_sb", [P, T])
        q_hi = sb("q_hi", [P, 2, T], F32R)
        q_lo = sb("q_lo", [P, 2, T], F32R)
        qbd_hi = sb("qbd_hi", [P, NBLK, HEADS, QB], F32R)
        qbd_lo = sb("qbd_lo", [P, NBLK, HEADS, QB], F32R)
        qbd_bf = sb("qbd_bf", [P, 2, HEADS, QB], BF16)
        kvs = sb("kvs", [P, NCAND, KVS])
        vals = sb("vals", [P, NCAND, 2, C])
        kt = sb("kt", [P, P])
        kt_hi = sb("kt_hi", [P, NCAND, P], F32R)
        kt_lo = sb("kt_lo", [P, NCAND, P], F32R)
        kt_bf = sb("kt_bf", [P, NCAND, P], BF16)
        ties = sb("ties", [P, P])
        beats = sb("beats", [P, P], BF16)
        wins = sb("wins", [P, 1])
        perm = sb("perm", [P, KEEP])
        mask = sb("mask", [P, NBLK, P], BF16)
        rowmax = sb("rowmax", [P, 2, PAIRS])
        maxmask = sb("maxmask", [P, 2, 4, P], BF16)
        probs = sb("probs", [P, 2, HEADS, QB])
        probs_space = probs[:].rearrange("p k h q -> p (k h q)")[:, 0:T]
        rden = sb("rden", [P, 2, QB])
        attn = sb("attn", [P, 2, 2, QB])
        z1 = sb("z1", [P, TILES, C])
        stats = sb("stats", [P, TILES, 6])
        mv = sb("mv", [P, TILES, 2])
        rstd = sb("rstd", [P, TILES])
        eps = sb("eps", [P, TILES])
        var = sb("var", [P, TILES])
        var2 = sb("var2", [P, TILES])
        minus_half = sb("minus_half", [P, TILES])
        x1 = sb("x1", [P, 2, TILES, C])
        x1t = sb("x1t", [P, 2, T])
        lmax = sb("lmax", [P, TILES])
        lsub = sb("lsub", [P, TILES, EXPERTS])
        lexp = sb("lexp", [P, TILES, EXPERTS])
        lsum = sb("lsum", [P, TILES])
        linv = sb("linv", [P, TILES])
        score = sb("score", [P, TILES, EXPERTS])
        better = sb("better", [P, TILES, EXPERTS, EXPERTS])
        equal = sb("equal", [P, TILES, EXPERTS, EXPERTS])
        rank8 = sb("rank8", [P, TILES, EXPERTS])
        gate = sb("gate", [P, TILES, EXPERTS])
        gate_rows = sb("gate_rows", [EXPERTS, T])
        gate_b = sb("gate_b", [P, EXPERTS, T])
        xe = sb("xe", [P, T])
        x_hi = sb("x_hi", [P, 2, T], F32R)
        x_lo = sb("x_lo", [P, 2, T], F32R)
        tanh_g = sb("tanh_g", [P, T])
        hid = sb("hid", [P, 2, T])
        z2 = sb("z2", [P, TILES, C])
        n_in, n_first = 2 * NE * HIDDEN, sum(w for _, w in FIRST_PARTS)
        gate_space = gate_b[:].rearrange("p e t -> p (e t)")
        w_in = gate_space[:, 0:n_in].rearrange("p (w e h) -> p w e h", w=2, e=NE)
        wo_in = gate_space[:, n_in:n_in + C]
        first_table = gate_space[:, n_in + C:n_in + C + n_first]
        for i, (n, w) in enumerate(FIRST_PARTS):
            tables[n] = first_table[:, i * P:i * P + w]
        stats2 = sb("stats2", [P, TILES, 6])
        mv2 = sb("mv2", [P, TILES, 2])
        rstd2 = sb("rstd2", [P, TILES])
        y_sb = sb("y_sb", [P, 2, TILES, C])

        bank_a = bank("bank_a")
        bank_b = bank("bank_b")
        bank_kv = bank("bank_kv")
        bank_o = bank("bank_o")
        bank_m = bank("bank_m")
        bank_g = bank("bank_g")
        bank_u = bank("bank_u")
        bank_f = bank("bank_f")

        first_in = sem("first_in")
        weights_in = sem("weights_in")
        xt_in = [sem("xt_in0"), sem("xt_in1")]
        xn_in = [sem("xn_in0"), sem("xn_in1")]
        qbd_hi_in = [sem("qbd_hi_in0"), sem("qbd_hi_in1")]
        qbd_lo_in = [sem("qbd_lo_in0"), sem("qbd_lo_in1")]
        gate_out = sem("gate_out")
        gate_in = [sem("gate_in0"), sem("gate_in1")]
        y_out = [sem("y_out0"), sem("y_out1")]
        tables_ready = sem("tables_ready")
        wo2_ready = sem("wo2_ready")
        zeroed = sem("zeroed")
        first_hi = sem("first_hi")
        first_lo = sem("first_lo")
        w_hi_ready = sem("w_hi_ready")
        w_lo_ready = sem("w_lo_ready")
        half_set = sem("half_set")
        ones_zeroed = sem("ones_zeroed")
        q_done = sem("q_done")
        kv_done = sem("kv_done")
        tp_done = sem("tp_done")
        count_done = sem("count_done")
        a_done = sem("a_done")
        b_done = sem("b_done")
        o_done = sem("o_done")
        y_done = sem("y_done")
        x1t_done = sem("x1t_done")
        logit_done = sem("logit_done")
        gatet_done = sem("gatet_done")
        g_done = sem("g_done")
        u_done = sem("u_done")
        ffn_done = sem("ffn_done")
        q_ready = sem("q_ready")
        vals_ready = sem("vals_ready")
        kt_ready = sem("kt_ready")
        qbf_ready = sem("qbf_ready")
        exp_done = sem("exp_done")
        x1t_ready = sem("x1t_ready")
        lexp_ready = sem("lexp_ready")
        gate_rows_ready = sem("gate_rows_ready")
        tanh_done = sem("tanh_done")
        maxmask_ready = [sem("maxmask_ready0"), sem("maxmask_ready1")]
        x_hi_ready = sem("x_hi_ready")
        kvs_ready = sem("kvs_ready")
        ties_done = sem("ties_done")
        beats_ready = sem("beats_ready")
        perm_ready = sem("perm_ready")
        mask_ready = sem("mask_ready")
        max_ready = sem("max_ready")
        weighted = sem("weighted")
        rden_done = sem("rden_done")
        attn_ready = sem("attn_ready")
        z1_ready = sem("z1_ready")
        stats_done = sem("stats_done")
        mv_ready = sem("mv_ready")
        x1_ready = sem("x1_ready")
        gate_step = sem("gate_step")
        lsub_ready = sem("lsub_ready")
        gate_ready = sem("gate_ready")
        gated_done = sem("gated_done")
        hid_ready = sem("hid_ready")
        z2_ready = sem("z2_ready")
        stats2_done = sem("stats2_done")
        mv2_ready = sem("mv2_ready")
        waited = sem("waited")
        res_ready = sem("res_ready")
        q_lo_ready = sem("q_lo_ready")
        kt_lo_ready = sem("kt_lo_ready")
        var_done = sem("var_done")
        rstd_ready = sem("rstd_ready")
        var2_done = sem("var2_done")
        rstd2_ready = sem("rstd2_ready")
        centred = sem("centred")
        y_ready = sem("y_ready")
        y_last_ready = sem("y_last_ready")
        xe_ready = sem("xe_ready")
        x_lo_ready = sem("x_lo_ready")

        N_FIRST, N_WEIGHTS = 6, 7
        N_MASKED = 2 * NBLK
        PART = NBLK // 2
        QBD_DMAS = HEADS
        GATES_FIRST = 2

        def wait(eng, s, count):
            if not (isinstance(count, int) and count <= 0):
                eng.wait_ge(s, count)

        class Seq:

            def __init__(self, n, half, d=0):
                self.n, self.half = n + (half + d) // 2, (half + d) % 2
                self.b = 2 * self.n + self.half

        LOOP_FROM, LOOP_TO = 2, B - 2

        def steps(eng, step):
            def peeled(b):
                step(b // 2, b % 2, lambda d: 0 <= b + d < B)

            for b in range(LOOP_FROM):
                peeled(b)
            with eng.Fori(0, (LOOP_TO - LOOP_FROM) // 2) as i:
                for half in range(2):
                    step(i + LOOP_FROM // 2, half, lambda d: True)
            for b in range(LOOP_TO, B + 2):
                peeled(b)

        def spread_first(eng, k, src, dst, done):
            eng.tensor_tensor(dst[:, k], src[:, 0, QB * k:QB * (k + 1)].unsqueeze(1).to_broadcast([P, HEADS, QB]),
                              tables["head"].unsqueeze(2).to_broadcast([P, HEADS, QB]), ALU.mult).then_inc(done, 1)

        LAST_FROM = 5

        def is_last(s, n):
            return isinstance(s.b, int) and (s.b == B - 1 or s.b == B - 2 and n >= LAST_FROM)

        def is_odd(s, n):
            return is_last(s, n) and (NE * s.b + n) % 2 == 1

        def banks_of(s, n):
            return (bank_a, bank_b) if is_odd(s, n) else (bank_g, bank_u)

        def tanh_of(s, n):
            return q_sb[:] if is_odd(s, n) else tanh_g[:]

        def x_of(s, n):
            if n == 0:
                return x1t[:, s.half, :]
            return probs_space if is_odd(s, n) else xe[:]

        block = ctx.enter_context(nc.Block())

        @block.sync
        def _(sp):
            first = [(wq_sb[:], wq_t), (bq_sb[:], bq), (wkvs_sb[:], w_kvs),
                     (bias_all[:], b_kvs.to_broadcast([P, KVS])), (table[:], consts),
                     (first_table, first_consts)]
            loads = [(bias_new[KEEP:P, :], b_kvs.to_broadcast([P - KEEP, KVS])),
                     (wo_in, wo_t), (bo_sb[:], bo.to_broadcast([P, C])), (gate_w[:], gate_t),
                     (w_in[:, 0], w1), (w_in[:, 1], w3), (w2_sb[:], w2)]

            def load_xt(s):
                sp.dma_start(xt_sb[:, s.half, :], x_t[s.b]).then_inc(xt_in[s.half], 16)

            def load_xn(s):
                sp.dma_start(xn_sb[:, s.half, :, :],
                             x[s.b].rearrange("(t p) c -> p t c", p=P)).then_inc(xn_in[s.half], 16)

            def hold(s, count):
                wait(sp, s, count)
                sp.sem_inc(waited, 1)

            def spread_queries(s, part):
                blocks = slice(part * PART, (part + 1) * PART)
                for src, dst, arrived in ((q_hi, qbd_hi, qbd_hi_in), (q_lo, qbd_lo, qbd_lo_in)):
                    for h in range(HEADS):
                        rows = slice(h * HS, (h + 1) * HS)
                        sp.dma_start(dst[rows, blocks, h, :].bitcast(F32),
                                     src[rows, s.half, :].bitcast(F32).rearrange("p (k q) -> p k q", q=QB)[:, blocks, :]
                                     ).then_inc(arrived[part], 16)

            load_xt(Seq(0, 0))
            for dst, src in first:
                sp.dma_start(dst, src).then_inc(first_in, 16)
            for dst, src in loads:
                sp.dma_start(dst, src).then_inc(weights_in, 16)
            load_xn(Seq(0, 0))
            for half in range(2):
                sp.sem_inc(y_out[half], 16)
            sp.wait_ge(q_lo_ready, 1)
            sp.wait_ge(zeroed, 2)

            def step(n, half, has):
                now, nxt, prev, prev2 = Seq(n, half), Seq(n, half, 1), Seq(n, half, -1), Seq(n, half, -2)
                if has(0):
                    hold(b_done, N_MASKED * now.b)
                    spread_queries(now, 1)
                if has(1):
                    hold(kv_done, NCAND * now.b)
                    load_xt(nxt)
                    hold(z1_ready, TILES * now.b)
                    load_xn(nxt)
                    hold(q_lo_ready, nxt.b + 1)
                    hold(b_done, N_MASKED * now.b + NBLK)
                    spread_queries(nxt, 0)
                if has(-2):
                    if has(0):
                        hold(y_ready, prev2.b + 1)
                    else:
                        hold(y_last_ready, prev2.b - (B - 3))
                    sp.dma_start(out[prev2.b].rearrange("(t p) c -> p t c", p=P),
                                 y_sb[:, prev2.half, :, :]).then_inc(y_out[prev2.half], 16)

            steps(sp, step)
            for half in range(2):
                sp.wait_ge(y_out[half], 16 * (B // 2) + 16)

        @block.gpsimd
        def _(pool):
            pool.memset(qbd_lo[:, PART:NBLK].bitcast(F32), 0.0).then_inc(zeroed, 1)
            pool.memset(minus_half[:], -0.5).then_inc(half_set, 1)
            pool.memset(eps[:], EPS).then_inc(half_set, 1)
            pool.wait_ge(half_set, 2)

            def split_q(s):
                pool.wait_ge(q_ready, s.b + 1)
                pool.tensor_tensor(q_lo[:, s.half, :], q_sb[:], q_hi[:, s.half, :],
                                   ALU.subtract).then_inc(q_lo_ready, 1)

            def split_keys(s, c):
                pool.wait_ge(kt_ready, NCAND * s.b + c)
                pool.tensor_tensor(kt_lo[:, c - 1, :], kt[:], kt_hi[:, c - 1, :],
                                   ALU.subtract).then_inc(kt_lo_ready, 1)

            split_q(Seq(0, 0))
            pool.wait_ge(q_lo_ready, 1)
            pool.wait_ge(first_in, 16 * N_FIRST)
            for k in range(PART):
                spread_first(pool, k, q_lo, qbd_lo, first_lo)
            split_keys(Seq(0, 0), 1)
            pool.wait_ge(weights_in, 16 * N_WEIGHTS)
            pool.wait_ge(w_hi_ready, 1)
            pool.tensor_tensor(w_lo[:], w_in, w_hi[:], ALU.subtract).then_inc(w_lo_ready, 1)

            pool.wait_ge(w_lo_ready, 1)

            def scale_x(s, n):
                if n == 1 + GATES_FIRST:
                    pool.wait_ge(gate_in[1], 16 * s.b + 16)
                if n == 1:
                    pool.wait_ge(gate_in[0], 16 * s.b + 16)
                if is_last(s, n):
                    pool.wait_ge(x_lo_ready, NE * s.b + n - 1)
                    pool.wait_ge(o_done, NBLK * B)
                else:
                    wait(pool, x_lo_ready, NE * s.b + (0 if n == 1 else n))
                pool.tensor_tensor(x_of(s, n), x1t[:, s.half, :], gate_b[:, ORDER[n], :], ALU.mult).then_inc(xe_ready, 1)

            def split_x(s, n):
                if is_last(s, n):
                    return
                src = x_of(s, n)
                half_ = (s.half + n) % 2
                pool.wait_ge(x_hi_ready, NE * s.b + n + 1)
                pool.tensor_tensor(x_lo[:, half_, :], src, x_hi[:, half_, :], ALU.subtract).then_inc(x_lo_ready, 1)

            def weigh(s):
                pool.wait_ge(exp_done, N_MASKED * s.b + 2)
                e = probs[0:QB, 0, :, :]
                pool.tensor_tensor(e, e, tables["times"][0:QB, :].unsqueeze(1).to_broadcast([QB, HEADS, QB]),
                                   ALU.mult).then_inc(weighted, 1)

            def finish(s, by_dve):
                pool.wait_ge(mv2_ready, s.b + 1)
                pool.tensor_tensor(var2[:], mv2[:, :, 1], eps[:], ALU.add).then_inc(var2_done, 1)
                pool.wait_ge(var2_done, s.b + 1)
                pool.tensor_tensor(rstd2[:], var2[:], minus_half[:], ALU.pow).then_inc(rstd2_ready, 1)
                if by_dve:
                    return
                pool.tensor_tensor(z2[:], z2[:], mv2[:, :, 0:1].to_broadcast([P, TILES, C]),
                                   ALU.subtract).then_inc(centred, 1)
                pool.wait_ge(rstd2_ready, s.b + 1)
                pool.wait_ge(centred, s.b + 1)
                pool.wait_ge(y_out[s.half], 16 * s.n + 16)
                pool.tensor_tensor(y_sb[:, s.half], z2[:], rstd2[:].unsqueeze(2).to_broadcast([P, TILES, C]),
                                   ALU.mult).then_inc(y_ready, 1)

            def gates_to_dram(s):
                pool.wait_ge(gate_rows_ready, s.b + 1)
                pool.sem_inc(waited, 1)
                pool.dma_start(gate_dram[s.half], gate_rows[:]).then_inc(gate_out, 16)

            def gates_to_all(s):
                pool.wait_ge(gate_out, 16 * s.b + 16)
                wait(pool, xe_ready, EXPERTS * s.b)
                if isinstance(s.b, int) and s.b == 0:
                    pool.wait_ge(wo2_ready, 1)
                pool.sem_inc(waited, 1)
                for part, e in enumerate((slice(0, GATES_FIRST), slice(GATES_FIRST, EXPERTS))):
                    pool.dma_start(gate_b[:, e, :].rearrange("p e t -> p (e t)"),
                                   gate_dram[s.half, e].rearrange("e t -> (e t)").partition_broadcast(P)
                                   ).then_inc(gate_in[part], 16)

            def step(n, half, has):
                now, nxt, prev, prev2 = Seq(n, half), Seq(n, half, 1), Seq(n, half, -1), Seq(n, half, -2)
                for k in range(NBLK):
                    if 0 < k < NCAND and has(0):
                        split_keys(now, k + 1)
                    if k == 5 and has(-1) and not has(0):
                        gates_to_dram(prev)
                    if k < 6 and has(-2) and not is_last(prev2, k + 3):
                        scale_x(prev2, k + 3)
                        split_x(prev2, k + 3)
                    if k < 5 and has(-2) and is_last(prev2, k + 4):
                        scale_x(prev2, k + 4)
                    if k == 1 and has(0):
                        weigh(now)
                    if k == 4 and has(1):
                        split_q(nxt)
                    if k == 0 and has(0):
                        pool.wait_ge(xn_in[now.half], 16 * now.n + 16)
                        pool.tensor_tensor(xn_sb[:, now.half], xn_sb[:, now.half],
                                           bo_sb[:].unsqueeze(1).to_broadcast([P, TILES, C]),
                                           ALU.add).then_inc(res_ready, 1)
                    if k == 2 and has(-1):
                        pool.wait_ge(mv_ready, prev.b + 1)
                        pool.tensor_tensor(var[:], mv[:, :, 1], eps[:], ALU.add).then_inc(var_done, 1)
                        pool.wait_ge(var_done, prev.b + 1)
                        pool.tensor_tensor(rstd[:], var[:], minus_half[:], ALU.pow).then_inc(rstd_ready, 1)
                    if k == 5 and has(-1):
                        if has(0):
                            gates_to_dram(prev)
                        gates_to_all(prev)
                        split_x(prev, 0)
                    if k in (6, 7) and has(-1):
                        scale_x(prev, k - 5)
                        split_x(prev, k - 5)
                    if k == 7 and has(-1) and is_last(prev, 3):
                        scale_x(prev, 3)
                    if k == 7 and has(1):
                        split_keys(nxt, 1)
                    if k == 7 and has(-2):
                        finish(prev2, not has(0))

            steps(pool, step)

        @block.tensor
        def _(pe):
            def mm(out_, lhs, rhs, start=True, stop=True):
                return pe.matmul(out_, lhs, rhs, start=start, stop=stop, skip_group_check=True)

            m_reader = [None]

            def use_bank_m(reader, count_after):
                if m_reader[0]:
                    pe.wait_ge(*m_reader[0])
                m_reader[0] = (reader, count_after)

            def queries(s):
                pe.wait_ge(xt_in[s.half], 16 * s.n + 16)
                use_bank_m(q_ready, s.b + 1)
                mm(bank_m[:], wq_sb[:], xt_sb[:, s.half, :]).then_inc(q_done, 1)

            def project(s, c):
                wait(pe, mask_ready, NCAND * s.b + c - 1)
                if c == 1:
                    mm(bank_kv[:, 0:KVS], xt_sb[:, s.half, 0:P], wkvs_sb[:]).then_inc(kv_done, 1)
                    return
                mm(bank_kv[KEEP:P, 0:KVS], xt_sb[:, s.half, QB * c:QB * (c + 1)], wkvs_sb[:])
                pe.wait_ge(perm_ready, (NCAND - 1) * s.b + c - 1)
                mm(bank_kv[0:KEEP, 0:KVS], perm[:], kvs[:, c - 2, :]).then_inc(kv_done, 1)

            def turn(s, c):
                pe.wait_ge(kvs_ready, NCAND * s.b + c)
                pe.transpose(bank_kv[:, 3 * P:4 * P], kvs[:, c - 1, 2 * C:KVS].to_broadcast([P, P]), ident)
                use_bank_m(kt_ready, NCAND * s.b + c)
                pe.transpose(bank_m[:, 0:P], kvs[:, c - 1, 0:C], ident).then_inc(tp_done, 1)

            def count(s, c):
                pe.wait_ge(beats_ready, NCAND * s.b + c)
                mm(bank_kv[:, 3 * P:4 * P], seen_bf[:], beats[:], stop=False)
                mm(bank_kv[:, 3 * P:4 * P], ident_bf[:], future_bf[:], start=False).then_inc(count_done, 1)

            def logits_a(s, k, g):
                c = max(k, 1) - 1
                if g == 0:
                    pe.wait_ge(qbf_ready, NBLK * s.b + k + 1)
                if k == 0 and g == 0:
                    pe.wait_ge(kt_ready, NCAND * s.b + 1)
                if k > 0 and g == 0:
                    pe.wait_ge(mask_ready, NCAND * s.b + k)
                    pe.wait_ge(kt_ready, NCAND * s.b + k)
                wait(pe, max_ready, N_MASKED * s.b + 2 * k + g)
                mm(bank_a[:], ident_bf[:], mask[:, k, :].unsqueeze(1).to_broadcast([P, 4, P]), stop=False)
                for p in range(4):
                    last = mm(bank_a[:, p * P:(p + 1) * P],
                              qbd_bf[:, k % 2, 8 * g + 2 * p:8 * g + 2 * p + 2, :].rearrange("p h q -> p (h q)"),
                              kt_bf[:, c, :], start=False, stop=p == 3)
                last.then_inc(a_done, 1)

            def logits_b(s, k, g):
                c = max(k, 1) - 1
                wait(pe, exp_done, N_MASKED * s.b + 2 * k + g)
                if isinstance(s.b, int) and s.b == 0 and k < PART:
                    pe.wait_ge(first_lo, k + 1)
                elif k % PART == 0 and g == 0:
                    pe.wait_ge(qbd_lo_in[k // PART], QBD_DMAS * 16 * (s.b + k // PART))
                pe.wait_ge(kt_lo_ready, NCAND * s.b + c + 1)
                hi, lo = (q_[:, k, 8 * g:8 * g + 8, :].rearrange("p h q -> p (h q)") for q_ in (qbd_hi, qbd_lo))
                mm(bank_b[:], kt_hi[:, c, :], hi, stop=False)
                mm(bank_b[:], kt_hi[:, c, :], lo, start=False, stop=False)
                mm(bank_b[:], kt_lo[:, c, :], hi, start=False, stop=False)
                pe.wait_ge(maxmask_ready[g], NBLK * s.b + k + 1)
                for p in range(4):
                    last = mm(bank_b[:, p * P:(p + 1) * P], maxmask[:, g, p, :], negid_bf[:],
                              start=False, stop=p == 3)
                last.then_inc(b_done, 1)

            def values(s, k):
                c = max(k, 1) - 1
                wait(pe, attn_ready, NBLK * s.b + k)
                pe.wait_ge(vals_ready, NCAND * s.b + c + 1)
                pe.wait_ge(exp_done, N_MASKED * s.b + 2 * k + 2)
                if k == 0:
                    pe.wait_ge(weighted, s.b + 1)
                for col in range(2):
                    for pair in range(2):
                        for g in range(GRP):
                            rows = slice(32 * g, 32 * g + 32)
                            lhs = ones_pair[:, pair, :] if col else vals[:, c, pair, rows]
                            h = 4 * g + 2 * pair
                            last = mm(bank_o[rows, P * col:P * (col + 1)], lhs,
                                      probs[:, k % 2, h:h + 2, :].rearrange("p h q -> p (h q)"),
                                      start=col == 0 and pair == 0, stop=pair == 1)
                last.then_inc(o_done, 1)

            def project_out(s, j):
                pe.wait_ge(attn_ready, NBLK * s.b + 2 * j + 2)
                if isinstance(s.b, int) and s.b == 0:
                    pe.wait_ge(wo2_ready, 1)
                use_bank_m(z1_ready, TILES * s.b + j + 1)
                for h in range(2):
                    last = mm(bank_m[:, 0:C], attn[:, h].rearrange("p k q -> p (k q)"), wo2[:, h, :],
                              start=h == 0, stop=h == 1)
                last.then_inc(y_done, 1)

            def turn_x1(s):
                pe.wait_ge(x1_ready, s.b + 1)
                use_bank_m(x1t_ready, s.b + 1)
                for t in range(TILES):
                    last = pe.transpose(bank_m[:, t * P:(t + 1) * P], x1[:, s.half, t, :], ident)
                last.then_inc(x1t_done, 1)

            def gate_logits(s):
                pe.wait_ge(x1t_ready, s.b + 1)
                use_bank_m(lsub_ready, s.b + 1)
                for t in range(TILES):
                    last = mm(bank_m[:, EXPERTS * t:EXPERTS * (t + 1)], x1t[:, s.half, t * P:(t + 1) * P], gate_w[:])
                last.then_inc(logit_done, 1)

            def turn_gates(s):
                pe.wait_ge(gate_ready, s.b + 1)
                use_bank_m(gate_rows_ready, s.b + 1)
                for t in range(TILES):
                    last = pe.transpose(bank_m[0:EXPERTS, t * P:(t + 1) * P], gate[:, t, :], ident)
                last.then_inc(gatet_done, 1)

            def up(s, n):
                e = ORDER[n]
                if is_last(s, n):
                    pe.wait_ge(hid_ready, NE * s.b + n - 1)
                    pe.wait_ge(max_ready, N_MASKED * B)
                    pe.wait_ge(exp_done, N_MASKED * B)
                else:
                    wait(pe, hid_ready, NE * s.b + n)
                pe.wait_ge(x_lo_ready, NE * s.b + n + 1)
                if isinstance(s.b, int) and s.b == 0 and n == 0:
                    pe.wait_ge(w_lo_ready, 1)
                hi, lo = x_hi[:, (s.half + n) % 2, :], x_lo[:, (s.half + n) % 2, :]
                for w, (bank_, done) in enumerate(zip(banks_of(s, n), (g_done, u_done))):
                    mm(bank_[:], w_hi[:, w, e, :], hi, stop=False)
                    mm(bank_[:], w_hi[:, w, e, :], lo, start=False, stop=False)
                    mm(bank_[:], w_lo[:, w, e, :], hi, start=False).then_inc(done, 1)

            def down(s, n):
                e = ORDER[n]
                pe.wait_ge(hid_ready, NE * s.b + n + 1)
                if n == 0:
                    wait(pe, z2_ready, s.b)
                for t in range(TILES):
                    last = mm(bank_f[:, t * C:(t + 1) * C], hid[:, (s.half + n) % 2, t * P:(t + 1) * P], w2_sb[:, e, :],
                              start=n == 0 and t == 0, stop=n == NE - 1)
                if n == NE - 1:
                    last.then_inc(ffn_done, 1)

            pe.wait_ge(first_in, 16 * N_FIRST)
            queries(Seq(0, 0))
            project(Seq(0, 0), 1)
            turn(Seq(0, 0), 1)
            pe.wait_ge(tables_ready, 1)

            def step(n, half, has):
                now, nxt, prev, prev2 = Seq(n, half), Seq(n, half, 1), Seq(n, half, -1), Seq(n, half, -2)
                if has(0):
                    m_reader[0] = (kt_ready, NCAND * now.b + 1)
                for k in range(NBLK):
                    if has(0):
                        logits_a(now, k, 0)
                    if k == 4 and has(-1) and not has(0):
                        gate_logits(prev)
                    if k < 7 and has(-2):
                        up(prev2, k + 2)
                    if k == 7 and has(-1):
                        up(prev, 1)
                    if k == 7 and has(1):
                        project(nxt, 1)
                    if k in (4, 6) and has(0):
                        project_out(now, k // 2 - 2)
                    if k in (0, 2) and has(-1):
                        project_out(prev, k // 2 + 2)
                    if has(0):
                        logits_a(now, k, 1)
                    if k == 4 and has(-1) and has(0):
                        gate_logits(prev)
                    if has(0) and k > 0:
                        logits_b(now, k - 1, 0)
                    if has(-1) and k == 0:
                        logits_b(prev, NBLK - 1, 0)
                    if has(0) and k < NCAND:
                        count(now, k + 1)
                    if k < 7 and has(-2):
                        down(prev2, k + 1)
                    if k == 7 and has(-1):
                        down(prev, 0)
                    if k == 4 and has(1):
                        queries(nxt)
                    if k == (5 if has(0) else 4) and has(-1):
                        turn_gates(prev)
                    if k == 7 and has(1):
                        turn(nxt, 1)
                    if k >= 2 and has(0):
                        values(now, k - 2)
                    if k < 2 and has(-1):
                        values(prev, NBLK - 2 + k)
                    if k == 6 and has(-1):
                        up(prev, 0)
                    if k == 6 and has(-2):
                        down(prev2, 8)
                    if k == 3 and has(-1):
                        turn_x1(prev)
                    if has(0) and k + 2 <= NCAND:
                        project(now, k + 2)
                    if has(0) and k > 0:
                        logits_b(now, k - 1, 1)
                    if has(-1) and k == 0:
                        logits_b(prev, NBLK - 1, 1)
                    if has(0) and k + 2 <= NCAND:
                        turn(now, k + 2)

            steps(pe, step)

        @block.scalar
        def _(act):
            act.wait_ge(first_in, 16 * N_FIRST)

            def queries(s):
                act.wait_ge(q_done, s.b + 1)
                wait(act, q_lo_ready, s.b)
                act.activation(q_sb[:], bank_m[:], ACT.Identity, bias=bq_sb[:])
                act.activation(q_hi[:, s.half, :], bank_m[:], ACT.Identity, bias=bq_sb[:]).then_inc(q_ready, 1)

            def round_queries(s, k):
                if isinstance(s.b, int) and s.b == 0 and k < PART:
                    act.wait_ge(first_hi, k + 1)
                elif k % PART == 0:
                    act.wait_ge(qbd_hi_in[k // PART], QBD_DMAS * 16 * (s.b + k // PART))
                wait(act, a_done, N_MASKED * s.b + 2 * k - 2)
                act.activation(qbd_bf[:, k % 2].rearrange("p h q -> p (h q)"),
                               qbd_hi[:, k].rearrange("p h q -> p (h q)"), ACT.Copy).then_inc(qbf_ready, 1)

            def pair_values(s, c):
                act.wait_ge(kvs_ready, NCAND * s.b + c)
                for pair in range(2):
                    last = act.activation(
                        vals[:, c - 1, pair].rearrange("p (g r i) -> p g r i", g=GRP, r=2)[:, :, pair, :],
                        kvs[:, c - 1, C:2 * C].rearrange("p (g r i) -> p g r i", g=GRP, r=2)[:, :, pair, :], ACT.Copy)
                last.then_inc(vals_ready, 1)

            def keys(s, c):
                act.wait_ge(tp_done, NCAND * s.b + c)
                wait(act, kt_lo_ready, NCAND * s.b + c - 1)
                act.activation(kt_bf[:, c - 1, :], bank_m[:, 0:P], ACT.Copy)
                act.activation(kt_hi[:, c - 1, :], bank_m[:, 0:P], ACT.Copy)
                act.activation(kt[:], bank_m[:, 0:P], ACT.Copy).then_inc(kt_ready, 1)

            def exp_gates(s):
                act.wait_ge(lsub_ready, s.b + 1)
                act.activation(lexp[:], lsub[:], ACT.Exp).then_inc(lexp_ready, 1)

            def exps(s, k, g):
                act.wait_ge(b_done, N_MASKED * s.b + 2 * k + g + 1)
                act.activation(probs[:, k % 2, 8 * g:8 * g + 8, :].rearrange("p h q -> p (h q)"),
                               bank_b[:], ACT.Exp, scale=SCALE).then_inc(exp_done, 1)

            def max_less_mask(s, k):
                act.wait_ge(max_ready, N_MASKED * s.b + 2 * k + 2)
                for p in range(4):
                    last = act.activation(maxmask[:, 1, p, :], mask[:, k, :], ACT.Identity,
                                          bias=rowmax[:, k % 2, 4 + p:5 + p], scale=-1.0)
                last.then_inc(maxmask_ready[1], 1)

            def tanh(s, n):
                act.wait_ge(g_done, NE * s.b + n + 1)
                act.activation(tanh_of(s, n), banks_of(s, n)[0][:], ACT.Tanh, scale=0.5).then_inc(tanh_done, 1)

            def upper_x(s, n):
                wait(act, u_done, NE * s.b + n - 1)
                if n > 0:
                    act.wait_ge(xe_ready, EXPERTS * s.b + n)
                else:
                    act.wait_ge(x1t_ready, s.b + 1)
                act.activation(x_hi[:, (s.half + n) % 2, :], x_of(s, n), ACT.Copy).then_inc(x_hi_ready, 1)

            queries(Seq(0, 0))
            round_queries(Seq(0, 0), 0)
            pair_values(Seq(0, 0), 1)
            keys(Seq(0, 0), 1)
            act.wait_ge(weights_in, 16 * N_WEIGHTS)
            act.activation(w_hi[:], w_in, ACT.Copy).then_inc(w_hi_ready, 1)

            def step(n, half, has):
                now, nxt, prev, prev2 = Seq(n, half), Seq(n, half, 1), Seq(n, half, -1), Seq(n, half, -2)
                for k in range(NBLK):
                    if k == 4 and has(-1) and not has(0):
                        exp_gates(prev)
                    if k < 6 and has(-2) and is_last(prev2, k + 3):
                        upper_x(prev2, k + 3)
                    if k < 7 and has(-2):
                        tanh(prev2, k + 2)
                    if k == 7 and has(-1):
                        tanh(prev, 1)
                    if k > 0 and has(0):
                        max_less_mask(now, k - 1)
                    if k == 0 and has(-1):
                        max_less_mask(prev, NBLK - 1)
                    if k < 6 and has(-2) and not is_last(prev2, k + 3):
                        upper_x(prev2, k + 3)
                    if k == 7 and has(-1):
                        upper_x(prev, 2)
                    for g in range(2):
                        if g == 1 and k == 6 and has(-1):
                            tanh(prev, 0)
                            upper_x(prev, 1)
                        if g == 1 and k < NBLK - 1 and k not in (3, 4) and has(0):
                            round_queries(now, k + 1)
                        if g == 1 and k == NBLK - 1 and has(1):
                            pair_values(nxt, 1)
                            keys(nxt, 1)
                            round_queries(nxt, 0)
                        if has(0) and k > 0:
                            exps(now, k - 1, g)
                        if has(-1) and k == 0:
                            exps(prev, NBLK - 1, g)
                        if g == 0 and k in (3, 4) and has(0):
                            round_queries(now, k + 1)
                        if g == 0 and k == 3 and has(-1):
                            act.wait_ge(x1t_done, prev.b + 1)
                            act.activation(x1t[:, prev.half, :], bank_m[:], ACT.Copy).then_inc(x1t_ready, 1)
                        if g == 0 and k == 4 and has(-1) and has(0):
                            exp_gates(prev)
                        if g == 0 and k == 4 and has(1):
                            queries(nxt)
                        if g == 0 and k == (5 if has(0) else 4) and has(-1):
                            act.wait_ge(gatet_done, prev.b + 1)
                            act.activation(gate_rows[:], bank_m[0:EXPERTS, :], ACT.Copy).then_inc(gate_rows_ready, 1)
                        if g == 1 and k == 5 and has(-1):
                            upper_x(prev, 0)
                    if has(0) and k + 2 <= NCAND:
                        pair_values(now, k + 2)
                        keys(now, k + 2)

            steps(act, step)

        @block.vector
        def _(dve):
            dve.memset(qbd_hi[:, PART:NBLK].bitcast(F32), 0.0).then_inc(zeroed, 1)
            dve.memset(vals[:], 0.0)
            dve.memset(ones_pair[:], 0.0).then_inc(ones_zeroed, 1)
            dve.memset(bias_new[0:KEEP, :], 0.0)
            dve.wait_ge(ones_zeroed, 1)
            for pair in range(2):
                dve.memset(ones_pair[:, pair, 16 * pair:16 * pair + 16], 1.0)
            dve.wait_ge(first_in, 16 * N_FIRST)
            dve.tensor_copy(ident_bf[:], ident)
            dve.tensor_scalar(negid_bf[:], ident, -1.0, None, ALU.mult)
            dve.tensor_copy(seen_bf[:], tables["seen"])
            dve.tensor_copy(future_bf[:], tables["future"])
            dve.tensor_scalar(mask[:, 0, :], tables["future0"], MASKED, None, ALU.mult)
            dve.sem_inc(tables_ready, 1)

            def candidates(s, c):
                dve.wait_ge(kv_done, NCAND * s.b + c)
                bias = bias_all if c == 1 else bias_new
                dve.tensor_tensor(kvs[:, c - 1, :], bank_kv[:, 0:KVS], bias[:], ALU.add).then_inc(kvs_ready, 1)

            def ranks(s, c):
                dve.wait_ge(tp_done, NCAND * s.b + c)
                own = kvs[:, c - 1, 2 * C:KVS]
                dve.scalar_tensor_tensor(ties[:], bank_kv[:, 3 * P:4 * P], own, tables["before"],
                                         ALU.is_equal, ALU.mult).then_inc(ties_done, 1)
                dve.wait_ge(ties_done, NCAND * s.b + c)
                dve.scalar_tensor_tensor(beats[:], bank_kv[:, 3 * P:4 * P], own, ties[:],
                                         ALU.is_lt, ALU.add, accum_out=wins[:]).then_inc(beats_ready, 1)
                if c < NCAND:
                    dve.wait_ge(beats_ready, NCAND * s.b + c)
                    dve.tensor_scalar(perm[:], tables["slot"], wins[:], None, ALU.is_equal).then_inc(perm_ready, 1)

            def masks(s, c):
                dve.wait_ge(count_done, NCAND * s.b + c)
                dve.tensor_scalar(mask[:, c, :], bank_kv[:, 3 * P:4 * P], KEEP - 0.5, MASKED,
                                  ALU.is_ge, ALU.mult).then_inc(mask_ready, 1)

            def maxima(s, k, g):
                dve.wait_ge(a_done, N_MASKED * s.b + 2 * k + g + 1)
                dve.tensor_reduce(rowmax[:, k % 2, 4 * g:4 * g + 4],
                                  bank_a[:].rearrange("p (a j) -> p a j", a=4), AX_X, ALU.max).then_inc(max_ready, 1)

            def max_less_mask(s, k):
                dve.wait_ge(max_ready, N_MASKED * s.b + 2 * k + 1)
                wait(dve, b_done, N_MASKED * s.b + 2 * k - 1)
                dve.sem_inc(waited, 1)
                for p in range(4):
                    last = dve.tensor_scalar(maxmask[:, 0, p, :], mask[:, k, :], -1.0, rowmax[:, k % 2, p:p + 1],
                                             ALU.mult, ALU.add)
                last.then_inc(maxmask_ready[0], 1)

            def normalise(s, k):
                dve.wait_ge(o_done, NBLK * s.b + k + 1)
                dve.reciprocal(rden[:].rearrange("p h q -> p (h q)"), bank_o[:, P:2 * P]).then_inc(rden_done, 1)
                dve.wait_ge(rden_done, NBLK * s.b + k + 1)
                dve.tensor_tensor(attn[:, :, k % 2, :], bank_o[:, 0:P].rearrange("p (h q) -> p h q", h=2),
                                  rden[:], ALU.mult).then_inc(attn_ready, 1)

            def residual(s, j):
                dve.wait_ge(y_done, TILES * s.b + j + 1)
                if j == 0:
                    dve.wait_ge(res_ready, s.b + 1)
                dve.tensor_tensor(z1[:, j, :], bank_m[:, 0:C], xn_sb[:, s.half, j, :], ALU.add).then_inc(z1_ready, 1)

            def layernorm_stats_of(s, tiles):
                dve.wait_ge(z1_ready, TILES * s.b + tiles[-1] + 1)
                for t in tiles:
                    dve.bn_stats(stats[:, t, :], z1[:, t, :]).then_inc(stats_done, 1)

            def layernorm_stats(s, z, z_sem, z_count, st, st_sem, mv_, mv_sem):
                if z is z1:
                    layernorm_stats_of(s, (2, 3))
                else:
                    dve.wait_ge(z_sem, z_count)
                    for t in range(TILES):
                        dve.bn_stats(st[:, t, :], z[:, t, :]).then_inc(st_sem, 1)
                dve.wait_ge(st_sem, TILES * s.b + TILES)
                dve.sem_inc(waited, 1)
                for t in range(TILES):
                    last = dve.bn_aggr(mv_[:, t, :], st[:, t, :])
                last.then_inc(mv_sem, 1)

            def finish_last(s):
                dve.wait_ge(rstd2_ready, s.b + 1)
                dve.wait_ge(y_out[s.half], 16 * s.n + 16)
                dve.sem_inc(waited, 1)
                for t in range(TILES):
                    last = dve.tensor_scalar(y_sb[:, s.half, t, :], z2[:, t, :], mv2[:, t, 0:1], rstd2[:, t:t + 1],
                                             ALU.subtract, ALU.mult)
                last.then_inc(y_last_ready, 1)

            def layernorm_apply(s):
                dve.wait_ge(rstd_ready, s.b + 1)
                for t in range(TILES):
                    last = dve.tensor_scalar(x1[:, s.half, t, :], z1[:, t, :], mv[:, t, 0:1], rstd[:, t:t + 1],
                                             ALU.subtract, ALU.mult)
                last.then_inc(x1_ready, 1)

            over_e = [P, TILES, EXPERTS]
            over_ee = [P, TILES, EXPERTS, EXPERTS]

            def gates_shift(s):
                logits = bank_m[:, 0:TILES * EXPERTS].rearrange("p (t e) -> p t e", e=EXPERTS)
                dve.wait_ge(logit_done, s.b + 1)
                dve.tensor_reduce(lmax[:], logits, AX_X, ALU.max).then_inc(gate_step, 1)
                dve.wait_ge(gate_step, 9 * s.b + 1)
                dve.tensor_tensor(lsub[:], logits, lmax[:].unsqueeze(2).to_broadcast(over_e),
                                  ALU.subtract).then_inc(lsub_ready, 1)

            def gate_chain(s, ins, at):
                ins.then_inc(gate_step, 1)
                dve.wait_ge(gate_step, 9 * s.b + at)

            def pairs_of(s):
                return (score[:].unsqueeze(2).to_broadcast(over_ee), score[:].unsqueeze(3).to_broadcast(over_ee))

            def gates_softmax(s):
                dve.wait_ge(lexp_ready, s.b + 1)
                gate_chain(s, dve.tensor_reduce(lsum[:], lexp[:], AX_X, ALU.add), 2)
                gate_chain(s, dve.reciprocal(linv[:], lsum[:]), 3)
                gate_chain(s, dve.tensor_tensor(score[:], lexp[:], linv[:].unsqueeze(2).to_broadcast(over_e),
                                                ALU.mult), 4)
                other, own = pairs_of(s)
                gate_chain(s, dve.tensor_tensor(equal[:], other, own, ALU.is_equal), 5)
                ee = equal[:].rearrange("p t e f -> p t (e f)")
                gate_chain(s, dve.tensor_tensor(ee, ee, tables["lower8"].unsqueeze(1).to_broadcast(
                    [P, TILES, EXPERTS ** 2]), ALU.mult), 6)

            def gates_choose(s):
                other, own = pairs_of(s)
                gate_chain(s, dve.tensor_tensor(better[:], other, own, ALU.is_gt), 7)
                gate_chain(s, dve.tensor_tensor(better[:], better[:], equal[:], ALU.add), 8)
                gate_chain(s, dve.tensor_reduce(rank8[:], better[:], AX_X, ALU.add), 9)
                dve.scalar_tensor_tensor(gate[:], rank8[:], 1.5, score[:], ALU.is_lt, ALU.mult).then_inc(gate_ready, 1)

            def lower_x(s, n):
                if not is_last(s, n):
                    return
                half_ = (s.half + n) % 2
                dve.wait_ge(x_hi_ready, NE * s.b + n + 1)
                dve.tensor_tensor(x_lo[:, half_, :], x_of(s, n), x_hi[:, half_, :],
                                  ALU.subtract).then_inc(x_lo_ready, 1)

            def hidden(s, n):
                dve.wait_ge(tanh_done, NE * s.b + n + 1)
                gated = tanh_of(s, n)
                bank_of_g, bank_of_u = banks_of(s, n)
                dve.scalar_tensor_tensor(gated, gated, 1.0, bank_of_g[:],
                                         ALU.add, ALU.mult).then_inc(gated_done, 1)
                dve.wait_ge(u_done, NE * s.b + n + 1)
                dve.wait_ge(gated_done, NE * s.b + n + 1)
                dve.scalar_tensor_tensor(hid[:, (s.half + n) % 2, :], gated, 0.5, bank_of_u[:],
                                         ALU.mult, ALU.mult).then_inc(hid_ready, 1)

            dve.wait_ge(q_ready, 1)
            spread_first(dve, 0, q_hi, qbd_hi, first_hi)
            candidates(Seq(0, 0), 1)
            for k in range(1, PART):
                spread_first(dve, k, q_hi, qbd_hi, first_hi)
            dve.wait_ge(weights_in, 16 * N_WEIGHTS)
            for h in range(2):
                last = dve.tensor_scalar(wo2[:, h, :], wo_in, tables["odd"][:, h:h + 1], None, ALU.mult)
            last.then_inc(wo2_ready, 1)

            def step(n, half, has):
                now, nxt, prev, prev2 = Seq(n, half), Seq(n, half, 1), Seq(n, half, -1), Seq(n, half, -2)
                for k in range(NBLK):
                    if has(0):
                        maxima(now, k, 0)
                    if has(0) and k < NCAND:
                        ranks(now, k + 1)
                    if k == 7 and has(1):
                        candidates(nxt, 1)
                    if k == 7 and has(-2):
                        dve.wait_ge(ffn_done, prev2.b + 1)
                        dve.tensor_tensor(z2[:], bank_f[:].rearrange("p (t c) -> p t c", c=C), x1[:, prev2.half],
                                          ALU.add).then_inc(z2_ready, 1)
                    if k in (4, 6) and has(0):
                        residual(now, k // 2 - 2)
                    if k in (0, 2) and has(-1):
                        residual(prev, k // 2 + 2)
                    if has(0):
                        maxima(now, k, 1)
                    if k == 4 and has(-1):
                        gates_shift(prev)
                    if k == 4 and has(-1) and not has(0):
                        gates_softmax(prev)
                        gates_choose(prev)
                    if k == 5 and has(-1) and has(0):
                        gates_choose(prev)
                    if has(0) and k == 5:
                        masks(now, k + 1)
                    if k == 2 and has(-1) and not has(0):
                        layernorm_stats(prev, z1, z1_ready, TILES * prev.b + TILES, stats, stats_done, mv, mv_ready)
                    if k == 3 and has(-1) and not has(0):
                        layernorm_apply(prev)
                    if k < 6 and has(-2):
                        lower_x(prev2, k + 3)
                    if k < 7 and has(-2):
                        hidden(prev2, k + 2)
                    if k >= 5 and has(-1):
                        lower_x(prev, k - 5)
                    if k == 7 and has(-1):
                        hidden(prev, 1)
                    if k == 2 and has(-1) and has(0):
                        layernorm_stats(prev, z1, z1_ready, TILES * prev.b + TILES, stats, stats_done, mv, mv_ready)
                    if k == 3 and has(-1) and has(0):
                        layernorm_apply(prev)
                    if k == 4 and has(-1) and has(0):
                        gates_softmax(prev)
                    if k == 0 and not has(-1) and has(-2) and not has(0):
                        finish_last(Seq(n, half, -3))
                    if k == 7 and has(-2):
                        layernorm_stats(prev2, z2, z2_ready, prev2.b + 1, stats2, stats2_done, mv2, mv2_ready)
                    if k == 7 and has(-2) and not has(-1):
                        finish_last(prev2)
                    if has(0) and k < NCAND and k != 5:
                        masks(now, k + 1)
                    if has(0):
                        max_less_mask(now, k)
                    if has(0) and k + 2 <= NCAND:
                        candidates(now, k + 2)
                    if k >= 2 and has(0):
                        normalise(now, k - 2)
                    if k == 6 and has(-1):
                        hidden(prev, 0)
                    if k == 6 and has(0):
                        layernorm_stats_of(now, (0, 1))
                    if k < 2 and has(-1):
                        normalise(prev, NBLK - 2 + k)

            steps(dve, step)


def kernel(**inputs):
    import concourse.bacc as bacc
    from concourse.bass_utils import run_bass_kernel_spmd

    a = {k.replace("L0_", ""): np.asarray(v) for k, v in inputs.items()}
    experts = {n: np.concatenate([a[f"ffn_{n}"], a[f"ffn_{n}s"]]) for n in ("w1", "w3", "w2")}
    arrays = {
        "x": a["attn_x"],
        "x_t": a["attn_x"].transpose(0, 2, 1),
        "wq_t": a["attn_Wq"].T,
        "bq": a["attn_bq"][:, None],
        "w_kvs": np.concatenate([a["attn_Wk"].T, a["attn_Wv"].T, a["attn_Wks"][:, None]], axis=1),
        "b_kvs": np.concatenate([a["attn_bk"], a["attn_bv"], a["attn_bks"].reshape(1)])[None, :],
        "wo_t": a["attn_Wo"].T,
        "bo": a["attn_bo"][None, :],
        "gate_t": a["ffn_gate_w"].T,
        "w1": experts["w1"].transpose(1, 0, 2),
        "w3": experts["w3"].transpose(1, 0, 2),
        "w2": experts["w2"].transpose(1, 0, 2),
        **dict(zip(("consts", "first_consts"), shape_constants())),
    }
    nc = bacc.Bacc("TRN2", target_bir_lowering=False, num_devices=1)
    arrays = {f"in_{n}": np.ascontiguousarray(v) for n, v in arrays.items()}
    args = [nc.dram_tensor(n, v.shape, mybir.dt.from_np(v.dtype), kind="ExternalInput").ap() for n, v in arrays.items()]
    args.append(nc.dram_tensor("out_y", (B, T, C), F32, kind="ExternalOutput").ap())
    post_ln_layer(nc, *args)
    r = run_bass_kernel_spmd(nc, [arrays], core_ids=[0])
    return r.results[0]["out_y"]
```
